# Optimizing a Trainium2 kernel written in Bass

```python
import numpy as np
import jax
import jax.numpy as jnp

def _softmax(x, axis=-1):
    return jax.nn.softmax(x, axis=axis)

def _gelu(x):
    return jax.nn.gelu(x, approximate=True)

def _silu(x):
    return jax.nn.silu(x)

def _sigmoid(x):
    return jax.nn.sigmoid(x)

def _layernorm(x, axis=-1, eps=1e-05):
    m = jnp.mean(x, axis=axis, keepdims=True)
    v = jnp.var(x, axis=axis, keepdims=True)
    return (x - m) / jnp.sqrt(v + eps)

def _scatter_add(tgt, idx, src, axis=0):
    return tgt.at[idx].add(src)

def _segment_sum(src, seg, n):
    return jax.ops.segment_sum(src, seg, n)
kernel_name = 'mk_vit_tower_postln_d1_tok_img256_r4_b70ae5'

def setup_inputs(seed: int=0):
    np.random.seed(seed)
    _w = jnp.asarray

    def _rec_inputs():
        import jax
        import jax.numpy as jnp
        _rk = jax.random.key(seed)
        x = -0.000596345 + 1.00056 * jax.random.normal(jax.random.fold_in(_rk, 1), (128, 64, 64, 3), jnp.float32)
        return x
    x = _rec_inputs()

    def _L0_tok_setup():
        import jax, jax.numpy as jnp
        import numpy as np
        M1 = 20
        M2 = 20

        def _spectral_conv(x, w):
            B, Cin, H, W = x.shape
            x_ft = jnp.fft.rfft2(x, norm='ortho')
            out = jnp.einsum('bixy,ioxy->boxy', x_ft[:, :, :M1, :M2], w.astype(x_ft.dtype))
            out_ft = jnp.zeros((B, w.shape[1], H, W // 2 + 1), dtype=x_ft.dtype)
            out_ft = out_ft.at[:, :, :M1, :M2].set(out)
            return jnp.fft.irfft2(out_ft, s=(H, W), norm='ortho')

        def _gelu(x):
            return jax.nn.gelu(x, approximate=False)
        key = jax.random.key(seed)
        ks = jax.random.split(key, 16)
        B, H, W, width = (16, 64, 64, 32)
        scale = 1.0 / (width * width)
        d = {}
        d['coords'] = jax.random.normal(ks[0], (B, H, W, 3), dtype=jnp.float32)
        d['fc0_w'] = jax.random.normal(ks[1], (3, width), dtype=jnp.float32) * 0.1
        d['fc0_b'] = jnp.zeros((width,), dtype=jnp.float32)
        for i in range(4):
            d[f'sw{i}'] = scale * jax.random.normal(ks[2 + i], (width, width, M1, M2), dtype=jnp.float32)
            d[f'cw{i}'] = jax.random.normal(ks[6 + i], (width, width), dtype=jnp.float32) * 0.1
            d[f'cb{i}'] = jnp.zeros((width,), dtype=jnp.float32)
        d['fc1_w'] = jax.random.normal(ks[10], (width, 64), dtype=jnp.float32) * 0.1
        d['fc1_b'] = jnp.zeros((64,), dtype=jnp.float32)
        d['fc2_w'] = jax.random.normal(ks[11], (64, 1), dtype=jnp.float32) * 0.1
        d['fc2_b'] = jnp.zeros((1,), dtype=jnp.float32)
        return d
    _L0_tok_all = _L0_tok_setup()
    _L0_tok_in = {k: v for k, v in _L0_tok_all.items() if k in ('fc0_w', 'fc0_b', 'sw0', 'cw0', 'cb0', 'sw1', 'cw1', 'cb1', 'sw2', 'cw2', 'cb2', 'sw3', 'cw3', 'cb3', 'fc1_w', 'fc1_b', 'fc2_w', 'fc2_b')}
    del _L0_tok_all

    def _L0_attn_setup():
        import jax, jax.numpy as jnp
        import numpy as np
        B, T, C, HR = (8, 1024, 64, 4)
        N_LAYER, LAYER_ID = (12, 3)
        HID = HR * C

        def _fancy_decay_first():
            r01 = LAYER_ID / (N_LAYER - 1)
            h = np.arange(C, dtype=np.float32)
            decay = -5.0 + 8.0 * (h / (C - 1)) ** (0.7 + 1.3 * r01)
            zig = (np.arange(1, C + 1) % 3 - 1).astype(np.float32) * 0.5
            first = np.float32(np.log(0.3)) + zig
            return (jnp.asarray(decay, jnp.float32), jnp.asarray(first, jnp.float32))

        def _ln(x, g, b):
            m = jnp.mean(x, axis=-1, keepdims=True)
            v = jnp.var(x, axis=-1, keepdims=True)
            return (x - m) * jax.lax.rsqrt(v + 1e-05) * g + b

        def _wkv(w, u, k, v):
            Bb, Tt, Cc = k.shape
            kT = jnp.swapaxes(k, 0, 1)
            vT = jnp.swapaxes(v, 0, 1)

            def step(carry, kv):
                p, q, o = carry
                kt, vt = kv
                no = jnp.maximum(o, u + kt)
                A = jnp.exp(o - no)
                E = jnp.exp(u + kt - no)
                y = (A * p + E * vt) / (A * q + E)
                no2 = jnp.maximum(w + o, kt)
                A2 = jnp.exp(w + o - no2)
                E2 = jnp.exp(kt - no2)
                return ((A2 * p + E2 * vt, A2 * q + E2, no2), y)
            init = (jnp.zeros((Bb, Cc), k.dtype), jnp.zeros((Bb, Cc), k.dtype), jnp.full((Bb, Cc), -1e+38, k.dtype))
            _, yT = jax.lax.scan(step, init, (kT, vT))
            return jnp.swapaxes(yT, 0, 1)
        key = jax.random.key(seed)
        ks = jax.random.split(key, 12)
        s = 0.02
        decay, first = _fancy_decay_first()
        return {'x': jax.random.normal(ks[0], (B, T, C), jnp.float32), 'Wk': jax.random.normal(ks[1], (C, C), jnp.float32) * s, 'Wv': jax.random.normal(ks[2], (C, C), jnp.float32) * s, 'Wr': jax.random.normal(ks[3], (C, C), jnp.float32) * s, 'Wo': jax.random.normal(ks[4], (C, C), jnp.float32) * s, 'Wk_ffn': jax.random.normal(ks[5], (C, HID), jnp.float32) * s, 'Wv_ffn': jax.random.normal(ks[6], (HID, C), jnp.float32) * s, 'Wr_ffn': jax.random.normal(ks[7], (C, C), jnp.float32) * s, 'g1': 1.0 + 0.1 * jax.random.normal(ks[8], (C,), jnp.float32), 'b1': 0.1 * jax.random.normal(ks[9], (C,), jnp.float32), 'g2': 1.0 + 0.1 * jax.random.normal(ks[10], (C,), jnp.float32), 'b2': 0.1 * jax.random.normal(ks[11], (C,), jnp.float32), 'spatial_decay': decay, 'spatial_first': first}
    _L0_attn_all = _L0_attn_setup()
    _L0_attn_in = {k: v for k, v in _L0_attn_all.items() if k in ('Wk', 'Wv', 'Wr', 'Wo', 'Wk_ffn', 'Wv_ffn', 'Wr_ffn', 'g1', 'b1', 'g2', 'b2', 'spatial_decay', 'spatial_first')}
    del _L0_attn_all

    def _L0_ffn_setup():
        import jax, jax.numpy as jnp
        import numpy as np
        C = 64
        HID = 256
        E = 8
        TEMP = 1.0
        key = jax.random.key(seed)
        ks = jax.random.split(key, 7)
        x = jax.random.normal(ks[0], (8, 4096, C), dtype=jnp.float32)
        W1 = jax.random.normal(ks[1], (C, HID), dtype=jnp.float32) * 0.02
        b1 = jnp.zeros((HID,), dtype=jnp.float32)
        Wg = jax.random.normal(ks[2], (HID, E), dtype=jnp.float32) * 0.02
        bg = jnp.zeros((E,), dtype=jnp.float32)
        Wd = jax.random.normal(ks[3], (E, HID, C), dtype=jnp.float32) * 0.02
        bd = jnp.zeros((E, C), dtype=jnp.float32)
        return {'x': x, 'W1': W1, 'b1': b1, 'Wg': Wg, 'bg': bg, 'Wd': Wd, 'bd': bd}
    _L0_ffn_all = _L0_ffn_setup()
    _L0_ffn_in = {k: v for k, v in _L0_ffn_all.items() if k in ('W1', 'b1', 'Wg', 'bg', 'Wd', 'bd')}
    del _L0_ffn_all
    return {'x': x, 'L0_tok_fc0_w': _L0_tok_in['fc0_w'], 'L0_tok_fc0_b': _L0_tok_in['fc0_b'], 'L0_tok_sw0': _L0_tok_in['sw0'], 'L0_tok_cw0': _L0_tok_in['cw0'], 'L0_tok_cb0': _L0_tok_in['cb0'], 'L0_tok_sw1': _L0_tok_in['sw1'], 'L0_tok_cw1': _L0_tok_in['cw1'], 'L0_tok_cb1': _L0_tok_in['cb1'], 'L0_tok_sw2': _L0_tok_in['sw2'], 'L0_tok_cw2': _L0_tok_in['cw2'], 'L0_tok_cb2': _L0_tok_in['cb2'], 'L0_tok_sw3': _L0_tok_in['sw3'], 'L0_tok_cw3': _L0_tok_in['cw3'], 'L0_tok_cb3': _L0_tok_in['cb3'], 'L0_tok_fc1_w': _L0_tok_in['fc1_w'], 'L0_tok_fc1_b': _L0_tok_in['fc1_b'], 'L0_tok_fc2_w': _L0_tok_in['fc2_w'], 'L0_tok_fc2_b': _L0_tok_in['fc2_b'], 'L0_attn_Wk': _L0_attn_in['Wk'], 'L0_attn_Wv': _L0_attn_in['Wv'], 'L0_attn_Wr': _L0_attn_in['Wr'], 'L0_attn_Wo': _L0_attn_in['Wo'], 'L0_attn_Wk_ffn': _L0_attn_in['Wk_ffn'], 'L0_attn_Wv_ffn': _L0_attn_in['Wv_ffn'], 'L0_attn_Wr_ffn': _L0_attn_in['Wr_ffn'], 'L0_attn_g1': _L0_attn_in['g1'], 'L0_attn_b1': _L0_attn_in['b1'], 'L0_attn_g2': _L0_attn_in['g2'], 'L0_attn_b2': _L0_attn_in['b2'], 'L0_attn_spatial_decay': _L0_attn_in['spatial_decay'], 'L0_attn_spatial_first': _L0_attn_in['spatial_first'], 'L0_ffn_W1': _L0_ffn_in['W1'], 'L0_ffn_b1': _L0_ffn_in['b1'], 'L0_ffn_Wg': _L0_ffn_in['Wg'], 'L0_ffn_bg': _L0_ffn_in['bg'], 'L0_ffn_Wd': _L0_ffn_in['Wd'], 'L0_ffn_bd': _L0_ffn_in['bd']}

def reference(x, L0_tok_fc0_w, L0_tok_fc0_b, L0_tok_sw0, L0_tok_cw0, L0_tok_cb0, L0_tok_sw1, L0_tok_cw1, L0_tok_cb1, L0_tok_sw2, L0_tok_cw2, L0_tok_cb2, L0_tok_sw3, L0_tok_cw3, L0_tok_cb3, L0_tok_fc1_w, L0_tok_fc1_b, L0_tok_fc2_w, L0_tok_fc2_b, L0_attn_Wk, L0_attn_Wv, L0_attn_Wr, L0_attn_Wo, L0_attn_Wk_ffn, L0_attn_Wv_ffn, L0_attn_Wr_ffn, L0_attn_g1, L0_attn_b1, L0_attn_g2, L0_attn_b2, L0_attn_spatial_decay, L0_attn_spatial_first, L0_ffn_W1, L0_ffn_b1, L0_ffn_Wg, L0_ffn_bg, L0_ffn_Wd, L0_ffn_bd):
    import jax
    import jax.numpy as jnp

    def _L0_tok_ref(coords, fc0_w, fc0_b, sw0, cw0, cb0, sw1, cw1, cb1, sw2, cw2, cb2, sw3, cw3, cb3, fc1_w, fc1_b, fc2_w, fc2_b):
        import jax, jax.numpy as jnp
        import numpy as np
        M1 = 20
        M2 = 20

        def _spectral_conv(x, w):
            B, Cin, H, W = x.shape
            x_ft = jnp.fft.rfft2(x, norm='ortho')
            out = jnp.einsum('bixy,ioxy->boxy', x_ft[:, :, :M1, :M2], w.astype(x_ft.dtype))
            out_ft = jnp.zeros((B, w.shape[1], H, W // 2 + 1), dtype=x_ft.dtype)
            out_ft = out_ft.at[:, :, :M1, :M2].set(out)
            return jnp.fft.irfft2(out_ft, s=(H, W), norm='ortho')

        def _gelu(x):
            return jax.nn.gelu(x, approximate=False)
        x = coords @ fc0_w + fc0_b
        x = jnp.transpose(x, (0, 3, 1, 2))
        for sw, cw, cb in ((sw0, cw0, cb0), (sw1, cw1, cb1), (sw2, cw2, cb2), (sw3, cw3, cb3)):
            x1 = _spectral_conv(x, sw)
            x2 = jnp.einsum('bchw,oc->bohw', x, cw) + cb[None, :, None, None]
            x = _gelu(x1 + x2)
        x = jnp.transpose(x, (0, 2, 3, 1))
        x = _gelu(x @ fc1_w + fc1_b)
        return (x @ fc2_w + fc2_b)[..., 0]

    def _L0_attn_ref(x, Wk, Wv, Wr, Wo, Wk_ffn, Wv_ffn, Wr_ffn, g1, b1, g2, b2, spatial_decay, spatial_first):
        import jax, jax.numpy as jnp
        import numpy as np
        B, T, C, HR = (8, 1024, 64, 4)
        N_LAYER, LAYER_ID = (12, 3)
        HID = HR * C

        def _fancy_decay_first():
            r01 = LAYER_ID / (N_LAYER - 1)
            h = np.arange(C, dtype=np.float32)
            decay = -5.0 + 8.0 * (h / (C - 1)) ** (0.7 + 1.3 * r01)
            zig = (np.arange(1, C + 1) % 3 - 1).astype(np.float32) * 0.5
            first = np.float32(np.log(0.3)) + zig
            return (jnp.asarray(decay, jnp.float32), jnp.asarray(first, jnp.float32))

        def _ln(x, g, b):
            m = jnp.mean(x, axis=-1, keepdims=True)
            v = jnp.var(x, axis=-1, keepdims=True)
            return (x - m) * jax.lax.rsqrt(v + 1e-05) * g + b

        def _wkv(w, u, k, v):
            Bb, Tt, Cc = k.shape
            kT = jnp.swapaxes(k, 0, 1)
            vT = jnp.swapaxes(v, 0, 1)

            def step(carry, kv):
                p, q, o = carry
                kt, vt = kv
                no = jnp.maximum(o, u + kt)
                A = jnp.exp(o - no)
                E = jnp.exp(u + kt - no)
                y = (A * p + E * vt) / (A * q + E)
                no2 = jnp.maximum(w + o, kt)
                A2 = jnp.exp(w + o - no2)
                E2 = jnp.exp(kt - no2)
                return ((A2 * p + E2 * vt, A2 * q + E2, no2), y)
            init = (jnp.zeros((Bb, Cc), k.dtype), jnp.zeros((Bb, Cc), k.dtype), jnp.full((Bb, Cc), -1e+38, k.dtype))
            _, yT = jax.lax.scan(step, init, (kT, vT))
            return jnp.swapaxes(yT, 0, 1)
        Tlen = x.shape[1]
        h = _ln(x, g1, b1)
        k = h @ Wk
        v = h @ Wv
        sr = jax.nn.sigmoid(h @ Wr)
        y = _wkv(spatial_decay / Tlen, spatial_first / Tlen, k, v)
        x = x + sr * y @ Wo
        h2 = _ln(x, g2, b2)
        kk = jnp.square(jax.nn.relu(h2 @ Wk_ffn))
        x = x + jax.nn.sigmoid(h2 @ Wr_ffn) * (kk @ Wv_ffn)
        return x

    def _L0_ffn_ref(x, W1, b1, Wg, bg, Wd, bd):
        import jax, jax.numpy as jnp
        import numpy as np
        C = 64
        HID = 256
        E = 8
        TEMP = 1.0
        orig_shape = x.shape
        xf = x.reshape(-1, orig_shape[-1])
        H = jax.nn.gelu(xf @ W1 + b1, approximate=False)
        probs = jax.nn.softmax((H @ Wg + bg) / TEMP, axis=-1)
        assign = jnp.argmax(probs, axis=-1)
        out = jnp.zeros_like(xf)
        for e in range(Wd.shape[0]):
            y = H @ Wd[e] + bd[e]
            sel = (assign == e)[:, None]
            out = out + jnp.where(sel, probs[:, e:e + 1] * y, 0.0)
        return out.reshape(orig_shape)
    h = _L0_tok_ref(x, L0_tok_fc0_w, L0_tok_fc0_b, L0_tok_sw0, L0_tok_cw0, L0_tok_cb0, L0_tok_sw1, L0_tok_cw1, L0_tok_cb1, L0_tok_sw2, L0_tok_cw2, L0_tok_cb2, L0_tok_sw3, L0_tok_cw3, L0_tok_cb3, L0_tok_fc1_w, L0_tok_fc1_b, L0_tok_fc2_w, L0_tok_fc2_b)
    h = _layernorm(h + _L0_attn_ref(h, L0_attn_Wk, L0_attn_Wv, L0_attn_Wr, L0_attn_Wo, L0_attn_Wk_ffn, L0_attn_Wv_ffn, L0_attn_Wr_ffn, L0_attn_g1, L0_attn_b1, L0_attn_g2, L0_attn_b2, L0_attn_spatial_decay, L0_attn_spatial_first), axis=-1)
    h = _layernorm(h + _L0_ffn_ref(h, L0_ffn_W1, L0_ffn_b1, L0_ffn_Wg, L0_ffn_bg, L0_ffn_Wd, L0_ffn_bd), axis=-1)
    return h

_drawn_inputs = setup_inputs


def setup_inputs(seed=0):
    import zlib

    import numpy as np

    out = dict(_drawn_inputs(seed))
    spreads = {'L0_tok_fc0_b': (0.0, 0.327),
     'L0_tok_cb0': (0.0, 0.1),
     'L0_tok_cb1': (0.0, 0.1),
     'L0_tok_cb2': (0.0, 0.1),
     'L0_tok_cb3': (0.0, 0.1),
     'L0_tok_fc1_b': (0.0, 0.1),
     'L0_ffn_b1': (0.0, 0.8),
     'L0_ffn_bg': (0.0, 0.1),
     'L0_ffn_bd': (0.0, 0.294)}
    factors = {'L0_tok_sw0': 8.0,
     'L0_tok_sw1': 8.0,
     'L0_tok_sw2': 8.0,
     'L0_tok_sw3': 8.0,
     'L0_attn_Wk': 8.0,
     'L0_attn_Wr': 6.193,
     'L0_attn_Wr_ffn': 5.554,
     'L0_attn_g1': 4.067,
     'L0_attn_spatial_first': 8.0,
     'L0_ffn_W1': 8.0,
     'L0_ffn_Wg': 8.0,
     'L0_ffn_Wd': 8.0}
    for name, (base, spread) in spreads.items():
        noise = np.random.default_rng([zlib.crc32(name.encode()), seed]).standard_normal(out[name].shape)
        drawn = base * np.exp(spread * noise) if base else spread * noise
        out[name] = jnp.asarray(drawn.astype(out[name].dtype))
    for name, factor in factors.items():
        out[name] = (out[name] * factor).astype(out[name].dtype)
    return out
```

```python
from contextlib import ExitStack

import numpy as np

import concourse.bass as bass
from concourse import mybir

F32 = mybir.dt.float32
ALU = mybir.AluOpType
ACT = mybir.ActivationFunctionType
AX = mybir.AxisListType

B, HW, CH, MODES, LAYERS = 128, 64, 32, 20, 4
G = 16
GROUPS = B // G
PAIRS, QUADS = G // 2, G // 4
J, HG = 4, 16
PIX = HG * HW
KR = 2 * MODES
HID, E = 256, 8
TP = HW // 2
T64, CT = HW, HW
N = HW * HW
NW = 96
NEG = -1e38


def dft_tables():
    k, n = np.arange(MODES), np.arange(HW)
    ang = 2 * np.pi * np.outer(n, k) / HW
    cos, sin = np.cos(ang) / 8, np.sin(ang) / 8
    over_w = np.zeros((128, NW))
    over_h = np.zeros((2, HW, 2, NW))
    w4, h6 = over_w[:, :80].reshape(2, HW, 2, 2, MODES), over_h[..., :80].reshape(2, HW, 2, 2, 2, MODES)
    back_h = np.zeros((128, 2, HG, J))
    back_w = np.zeros((128, 2, HW))
    twice = np.where(k == 0, 1.0, 2.0)[:, None]
    for i in range(2):
        w4[i, :, i, 0], w4[i, :, i, 1] = cos, -sin
        h6[i, :, 0, i, 0], h6[i, :, 0, i, 1] = cos, -sin
        h6[i, :, 1, i, 0], h6[i, :, 1, i, 1] = sin, cos
        back_h[KR * i:KR * i + KR, i] = np.concatenate([cos.T, -sin.T]).reshape(KR, J, HG).transpose(0, 2, 1)
        back_w[64 * i:64 * i + KR, i] = np.concatenate([twice * cos.T, -twice * sin.T])
    return {"t_over_w": over_w, "t_over_h": over_h.reshape(128, 2 * NW), "t_back_h": back_h.reshape(128, 128),
            "t_back_w": back_w.reshape(128, 128), "t_ident": np.eye(128)}


def tokenizer(nc, t):
    with ExitStack() as ctx:
        def sem(name):
            return ctx.enter_context(nc.semaphore(name))

        WORDS = 53200
        arena = ctx.enter_context(nc.sbuf_tensor("arena", [128, WORDS], F32))
        ps = ctx.enter_context(nc.psum_tensor("ps", [128, 8, 512], F32))
        top = [0]

        def take(n):
            top[0] += n
            assert top[0] <= WORDS, top
            return arena[:, top[0] - n:top[0]]

        ident = take(128)
        over_w, over_h, back_h, back_w = take(NW), take(2 * NW), take(128), take(128)
        cw, cb = take(128), take(1)
        fc0_w, fc0_b, fc1_w, fc1_b, fc2_w, fc2_b = take(128), take(1), take(256), take(1), take(252), take(1)
        x = take(G * PIX)
        T = take(2 * 2048)
        gel = T[:, 0:2048]
        ht = T[:, 2048:2560]
        VR = 64 + KR
        VROWS = VR * CH
        ybase = top[0]
        Y = take(2 * VROWS + 4096)
        V = [arena[:, ybase + i * VROWS:ybase + (i + 1) * VROWS] for i in range(2)]
        F2 = take(2 * 1280)
        Z = [arena[:, ybase + 2 * VROWS:ybase + 2 * VROWS + 4096],
             arena[:, top[0] - 2560:top[0] - 2560 + 4096]]
        Xt = take(3 * 1280)
        S = take(5 * MODES * CH)
        Sn = take(5 * MODES * CH)
        W = take(5 * 8 * 128)
        gate_in, gate_out = take(1), take(1)
        xin = take(2 * 1024)

        NCONST = 5 + 3 * J + 4 + 1
        consts = sem("consts")
        zeroed, gated = sem("zeroed"), sem("gated")
        x_ready, tp_ps, t_sb, y_ps, y_sb = sem("x_ready"), sem("tp_ps"), sem("t_sb"), sem("y_ps"), sem("y_sb")
        f2_ps, f2_sb, xt_sb = sem("f2_ps"), sem("f2_sb"), sem("xt_sb")
        w_loaded = [sem(f"w_loaded{a}") for a in range(5)]
        mix_ps, s_sb, sn_sb = sem("mix_ps"), sem("s_sb"), sem("sn_sb")
        v_loaded = [sem(f"v_loaded{i}") for i in range(4)]
        z_ps, z_sb, o_ps, layer_w = sem("z_ps"), sem("z_sb"), sem("o_ps"), sem("layer_w")
        xin_loaded = [sem("xin_loaded0"), sem("xin_loaded1")]
        fc0_ps, fc1_ps, g_sb, fc2_ps = sem("fc0_ps"), sem("fc1_ps"), sem("g_sb"), sem("fc2_ps")
        ht_sb, h_stored = sem("ht_sb"), sem("h_stored")

        block = ctx.enter_context(nc.Block())

        def bank(i):
            return ps[:, i, :]

        T_RING, Y_RING, Z_RING = (0, 1, 4, 5), (2, 3, 6, 7), (2, 3, 0, 1)

        def bank8(i):
            return ps[:, i, :].rearrange("p (h w) -> p h w", h=8)

        def xcols(im, b):
            c0 = im // 2 * 2048
            return x[:, c0:c0 + 2048].rearrange("p (h i w) -> p i h w", h=HG, i=2)[:, im % 2, 8 * b:8 * b + 8, :]

        def load_v(eng, it, half, gate):
            eng.wait_ge(s_sb, it * 15 + 15)
            eng.wait_ge(sn_sb, it * 15 + 15)
            gate(it, 0)
            for qd in range(QUADS):
                if qd >= 2:
                    eng.wait_ge(z_ps, it * 32 + 8 * (qd - 1))
                    gate(it, qd - 1)
                for i in range(2):
                    im = 4 * qd + 2 * half + i
                    for rr, kr, srct, ri in ((0, 0, S, 0), (0, 1, S, 1), (1, 0, S, 1), (1, 1, Sn, 0)):
                        p0 = 16 * ri + im
                        src = srct[p0:p0 + 97:32, :].rearrange("p (a f) -> p a f", a=5)
                        r0 = KR * half + MODES * kr
                        c0 = (i * 64 + rr * MODES) * CH
                        eng.dma_start(V[qd % 2][r0:r0 + MODES, c0:c0 + MODES * CH],
                                      src).then_inc(v_loaded[2 * half + qd % 2], 16)

        @block.gpsimd
        def _(pool):
            def gate(it, i):
                pool.wait_ge(gated, it * 3 + i + 1)
                nc.gpsimd.tensor_tensor(gate_out, gate_in, gate_in, ALU.add).then_inc(gated, 1)

            nc.gpsimd.memset(gate_in, 0.0).then_inc(gated, 1)
            with pool.Fori(0, GROUPS) as g:
                with pool.Fori(0, LAYERS) as l:
                    load_v(pool, g * LAYERS + l, 1, gate)

        @block.sync
        def _(sp):
            for dst, src in ((ident, t["t_ident"]), (over_w, t["t_over_w"]), (over_h, t["t_over_h"]),
                             (back_h, t["t_back_h"]), (back_w, t["t_back_w"])):
                sp.dma_start(dst, src).then_inc(consts, 16)
            sp.wait_ge(zeroed, 1)
            for j in range(J):
                sp.dma_start(fc0_w[3 * j:3 * j + 3, 32 * j:32 * j + 32], t["L0_tok_fc0_w"]).then_inc(consts, 16)
                sp.dma_start(fc0_b[32 * j:32 * j + 32, :], t["L0_tok_fc0_b"]).then_inc(consts, 16)
                s, jj = divmod(j, 2)
                sp.dma_start(fc1_w[32 * j:32 * j + 32, 128 * s + 64 * jj:128 * s + 64 * jj + 64],
                             t["L0_tok_fc1_w"]).then_inc(consts, 16)
            for jj in range(2):
                sp.dma_start(fc1_b[64 * jj:64 * jj + 64, :], t["L0_tok_fc1_b"]).then_inc(consts, 16)
                sp.dma_start(fc2_w[64 * jj:64 * jj + 64, 124 + 4 * jj:125 + 4 * jj], t["L0_tok_fc2_w"]).then_inc(consts, 16)
            sp.dma_start(fc2_b, t["L0_tok_fc2_b"].to_broadcast([128, 1])).then_inc(consts, 16)

            with sp.Fori(0, GROUPS) as g:
                for im in range(G):
                    if im >= 2:
                        sp.wait_ge(fc0_ps, g * 32 + 2 * (im - 1))
                    sp.dma_start(xin[0:12, im % 2 * 1024:(im % 2 + 1) * 1024],
                                 t["x"][g, im]).then_inc(xin_loaded[im % 2], 16)
                with sp.Fori(0, LAYERS) as l:
                    it = g * LAYERS + l
                    sp.wait_ge(x_ready, g * 160 + l * 32 + 32)
                    for j in range(J):
                        q = slice(32 * j, 32 * j + 32)
                        sp.dma_start(cw[q, q], t["cw"][l]).then_inc(layer_w, 16)
                        sp.dma_start(cb[q, :], t["cb"][l]).then_inc(layer_w, 16)
                    for n in range(15):
                        tt, a = divmod(n, 5)
                        if n >= 5:
                            sp.wait_ge(mix_ps, it * 15 + n - 4)
                        for q in range(4 if tt < 2 else 2):
                            dst = W[32 * q:32 * q + 32, a * 1024:(a + 1) * 1024].rearrange("p (m f) -> p m f", m=8)
                            sp.dma_start(dst[:, :, 32 * q:32 * q + 32],
                                         t["sw"][l, 4 * tt + q, a]).then_inc(w_loaded[a], 16)
                    load_v(sp, it, 0, lambda it, i: None)
                sp.wait_ge(ht_sb, g + 1)
                for i in range(2):
                    sp.dma_start(t["hs"][g, :, i], ht[:, 256 * i:256 * i + 256]).then_inc(h_stored, 16)
            sp.wait_ge(h_stored, GROUPS * 32)

        @block.tensor
        def _(pe):
            mm = nc.tensor.matmul
            pe.wait_ge(consts, 16 * NCONST)
            with pe.Fori(0, GROUPS) as g:
                for n in range(2 * G):
                    im, b = divmod(n, 2)
                    if b == 0:
                        pe.wait_ge(xin_loaded[im % 2], g * 128 + 16 * (im // 2 + 1))
                    if n >= 4:
                        pe.wait_ge(x_ready, g * 160 + n - 3)
                    c0 = im % 2 * 1024 + b * 512
                    mm(bank(4 + n % 4), fc0_w, xin[:, c0:c0 + 512],
                       start=True, stop=True).then_inc(fc0_ps, 1)

                with pe.Fori(0, LAYERS) as l:
                    it = g * LAYERS + l

                    def turn(pr):
                        xp = x[:, pr * 2048:(pr + 1) * 2048].rearrange("p (h m) -> p h m", h=HG)
                        pe.wait_ge(x_ready, g * 160 + l * 32 + 4 * (pr + 1))
                        for k in range(4):
                            n = 4 * pr + k
                            if n == 2:
                                pe.wait_ge(x_ready, g * 160 + l * 32 + 32)
                            if n >= 4:
                                pe.wait_ge(t_sb, it * 32 + n - 3)
                            for h in range(4):
                                m = nc.tensor.transpose(bank(T_RING[n % 4])[:, 128 * h:128 * h + 128],
                                                        xp[:, 4 * k + h, :], ident)
                            m.then_inc(tp_ps, 1)

                    def dft_w(pr):
                        pe.wait_ge(t_sb, it * 32 + 4 * (pr + 1))
                        for k in range(4):
                            n = 4 * pr + k
                            if n >= 4:
                                pe.wait_ge(y_sb, it * 32 + n - 3)
                            for c in range(4):
                                c0 = pr % 2 * 2048 + (4 * k + c) * 128
                                m = mm(bank(Y_RING[n % 4])[:, NW * c:NW * c + NW], T[:, c0:c0 + 128], over_w,
                                       start=True, stop=True)
                            m.then_inc(y_ps, 1)

                    turn(0)
                    for pr in range(PAIRS):
                        if pr + 1 < PAIRS:
                            turn(pr + 1)
                        dft_w(pr)

                    pe.wait_ge(y_sb, it * 32 + 32)
                    for n in range(12):
                        tt, k = divmod(n, 4)
                        M, w = (128, NW) if tt < 2 else (64, 80)
                        if n >= 2:
                            pe.wait_ge(f2_sb, it * 12 + n - 1)
                        for c in range(4):
                            for ri in range(2):
                                c0 = ((4 * k + c) * 2 + ri) * MODES * G + tt * 128
                                m = mm(bank(4 + n % 2)[0:M, NW * c:NW * c + w], Y[:, c0:c0 + M],
                                       over_h[:, NW * ri:NW * ri + w], start=ri == 0, stop=ri == 1)
                        m.then_inc(f2_ps, 1)

                    for n in range(15):
                        tt, a = divmod(n, 5)
                        P = 128 if tt < 2 else 64
                        pe.wait_ge(xt_sb, it * 3 + tt + 1)
                        pe.wait_ge(w_loaded[a], it * 160 + (64, 128, 160)[tt])
                        if n >= 2:
                            pe.wait_ge(s_sb, it * 15 + n - 1)
                        for b in range(4):
                            for k2 in range(2):
                                c0 = tt * 1280 + (5 * b + a) * 64
                                lhsT = Xt[:, c0 + 32 * k2:c0 + 32 * k2 + 32]
                                o = bank(6 + n % 2)[32 * b:32 * b + 32, 0:2 * P].rearrange("p (q k o) -> p q k o", k=2, o=CH)
                                c1 = a * 1024 + (2 * b + k2) * 128
                                m = mm(o[:, :, k2], lhsT, W[:, c1:c1 + P], start=True, stop=True)
                        m.then_inc(mix_ps, 1)

                    def back_over_h(qd):
                        for half in range(2):
                            pe.wait_ge(v_loaded[2 * half + qd % 2], it * 256 + 128 * (qd // 2 + 1))
                        for k in range(8):
                            n = 8 * qd + k
                            if n >= 4:
                                pe.wait_ge(z_sb, it * 32 + n - 3)
                            for c in range(4):
                                m = mm(bank(Z_RING[n % 4])[0:VR, 128 * c:128 * c + 128],
                                       V[qd % 2][:, 4 * k + c:VROWS:CH], back_h, start=True, stop=True)
                            m.then_inc(z_ps, 1)

                    def channels(n):
                        mm(bank(4 + n % 4), cw, x[:, 512 * n:512 * n + 512], start=True, stop=False)

                    def finish(pr):
                        if pr % 2 == 0:
                            pe.wait_ge(z_sb, it * 32 + 4 * (pr + 2))
                        for k in range(4):
                            n = 4 * pr + k
                            if n >= 4:
                                pe.wait_ge(x_ready, g * 160 + (l + 1) * 32 + n - 3)
                                channels(n)
                            for h in range(4):
                                z0 = pr % 2 * 2048 + (4 * k + h) * 128
                                m = mm(bank(4 + n % 4)[:, 128 * h:128 * h + 128],
                                       Z[pr // 2 % 2][0:VR, z0:z0 + 128], back_w[0:VR, :], start=False, stop=h == 3)
                            m.then_inc(o_ps, 1)

                    pe.wait_ge(layer_w, it * 128 + 128)
                    pe.wait_ge(s_sb, it * 15 + 15)
                    for n in range(4):
                        channels(n)
                    back_over_h(0)
                    for qd in range(QUADS):
                        if qd + 1 < QUADS:
                            back_over_h(qd + 1)
                        finish(2 * qd)
                        finish(2 * qd + 1)

                def fc2(n):
                    pr, k, s = n // 8, n // 2 % 4, n % 2
                    pe.wait_ge(g_sb, g * 64 + n + 1)
                    c0 = 124 - (16 * pr + 8 * s + k)
                    mm(bank(2), fc2_w[:, c0:c0 + 128], gel[:, n % 4 * 512:n % 4 * 512 + 512],
                       start=n == 0, stop=n == 4 * G - 1).then_inc(fc2_ps, 1)

                pe.wait_ge(x_ready, g * 160 + 160)
                for n in range(4 * G):
                    if n >= 4:
                        pe.wait_ge(g_sb, g * 64 + n - 3)
                    mm(bank(4 + n % 4), fc1_w[:, 128 * (n % 2):128 * (n % 2) + 128],
                       x[:, 512 * (n // 2):512 * (n // 2) + 512], start=True, stop=True).then_inc(fc1_ps, 1)
                    if n >= 2:
                        fc2(n - 2)
                fc2(4 * G - 2)
                fc2(4 * G - 1)
                pe.wait_ge(ht_sb, g + 1)

        @block.scalar
        def _(act):
            act.wait_ge(consts, 16 * NCONST)
            with act.Fori(0, GROUPS) as g:
                for n in range(2 * G):
                    act.wait_ge(fc0_ps, g * 32 + n + 1)
                    nc.scalar.activation(xcols(n // 2, n % 2), bank8(4 + n % 4), ACT.Identity,
                                         bias=fc0_b).then_inc(x_ready, 1)
                with act.Fori(0, LAYERS) as l:
                    it = g * LAYERS + l
                    for n in range(32):
                        pr, k = divmod(n, 4)
                        act.wait_ge(y_ps, it * 32 + n + 1)
                        dst = Y[:, k * 4 * 640:(k + 1) * 4 * 640].rearrange("p (c k i) -> p c i k", c=4, k=KR)
                        src = bank(Y_RING[n % 4])[:, 0:4 * NW].rearrange("p (c m) -> p c m", c=4)[:, :, 0:80].rearrange(
                            "p c (i k) -> p c i k", i=2)
                        nc.scalar.activation(dst[:, :, 2 * pr:2 * pr + 2], src, ACT.Identity).then_inc(y_sb, 1)
                    for n in range(15):
                        tt, a = divmod(n, 5)
                        w = 256 if tt < 2 else 128
                        c0 = a * 640 + 256 * tt
                        act.wait_ge(s_sb, it * 15 + n + 1)
                        nc.scalar.mul(Sn[:, c0:c0 + w], S[:, c0:c0 + w], -1.0).then_inc(sn_sb, 1)
                    act.wait_ge(layer_w, it * 128 + 128)
                    for n in range(32):
                        act.wait_ge(o_ps, it * 32 + n + 1)
                        nc.scalar.activation(x[:, 512 * n:512 * n + 512], bank(4 + n % 4), ACT.Gelu,
                                             bias=cb).then_inc(x_ready, 1)
                for n in range(4 * G):
                    act.wait_ge(fc1_ps, g * 64 + n + 1)
                    if n >= 4:
                        act.wait_ge(fc2_ps, g * 64 + n - 3)
                    nc.scalar.activation(gel[:, n % 4 * 512:n % 4 * 512 + 512], bank(4 + n % 4), ACT.Gelu,
                                         bias=fc1_b).then_inc(g_sb, 1)

        @block.vector
        def _(dve):
            nc.vector.memset(W, 0.0)
            nc.vector.memset(xin, 0.0)
            nc.vector.memset(Xt[64:128, 2 * 1280:3 * 1280], 0.0)
            nc.vector.memset(cw, 0.0)
            nc.vector.memset(fc1_w, 0.0)
            nc.vector.memset(fc2_w, 0.0)
            nc.vector.memset(fc0_w, 0.0).then_inc(zeroed, 1)
            dve.wait_ge(consts, 16 * NCONST)
            with dve.Fori(0, GROUPS) as g:
                with dve.Fori(0, LAYERS) as l:
                    it = g * LAYERS + l
                    for n in range(32):
                        pr, k = divmod(n, 4)
                        if k == 0 and pr >= 2:
                            dve.wait_ge(y_ps, it * 32 + 4 * (pr - 1))
                        dve.wait_ge(tp_ps, it * 32 + n + 1)
                        dst = T[:, pr % 2 * 2048:(pr % 2 + 1) * 2048].rearrange("p (c j h) -> p h j c", c=CH, j=J)
                        src = bank(T_RING[n % 4]).rearrange("p (h j c) -> p h j c", h=4, j=J)
                        nc.vector.tensor_copy(dst[:, 4 * k:4 * k + 4], src).then_inc(t_sb, 1)
                    for n in range(12):
                        tt, k = divmod(n, 4)
                        M = 128 if tt < 2 else 64
                        if n == 8:
                            dve.wait_ge(xt_sb, it * 3 + 1)
                        dve.wait_ge(f2_ps, it * 12 + n + 1)
                        c0 = tt % 2 * 1280
                        dst = F2[0:M, c0:c0 + 1280].rearrange("p (k g c) -> p g c k", g=HG, c=2)
                        src = bank(4 + n % 2)[0:M, 0:4 * NW].rearrange("p (g m) -> p g m", g=4)[:, :, 0:80].rearrange(
                            "p g (c k) -> p g c k", c=2)
                        nc.vector.tensor_copy(dst[:, 4 * k:4 * k + 4], src).then_inc(f2_sb, 1)
                        if k == 3:
                            dve.wait_ge(f2_sb, it * 12 + n + 1)
                            dst = Xt[0:M, tt * 1280:(tt + 1) * 1280].rearrange("p (x k r i) -> p r x k i",
                                                                               x=MODES, k=2, r=2)
                            for ri in range(2):
                                m = nc.vector.transpose(dst[:, ri], F2[0:M, c0 + 640 * ri:c0 + 640 * ri + 640])
                            m.then_inc(xt_sb, 1)
                    dve.wait_ge(xt_sb, it * 3 + 3)
                    for n in range(15):
                        tt, a = divmod(n, 5)
                        w = 256 if tt < 2 else 128
                        dve.wait_ge(mix_ps, it * 15 + n + 1)
                        c0 = a * 640 + 256 * tt
                        nc.vector.tensor_copy(S[:, c0:c0 + w], bank(6 + n % 2)[:, 0:w]).then_inc(s_sb, 1)
                    for n in range(32):
                        qd, k = divmod(n, 8)
                        if k == 0 and qd >= 2:
                            dve.wait_ge(o_ps, it * 32 + 8 * (qd - 1))
                        dve.wait_ge(z_ps, it * 32 + n + 1)
                        dst = Z[qd % 2][0:VR, :].rearrange("p (r h o) -> p o r h", r=2, o=CH)
                        src = bank(Z_RING[n % 4])[0:VR, :].rearrange("p (o r h) -> p o r h", o=4, r=2)
                        nc.vector.tensor_copy(dst[:, 4 * k:4 * k + 4], src).then_inc(z_sb, 1)
                dve.wait_ge(fc2_ps, g * 64 + 64)
                nc.vector.tensor_scalar(ht.rearrange("p (i h w) -> p h i w", i=2, h=4),
                                        bank(2).rearrange("p (h i w) -> p h i w", h=4, i=2),
                                        fc2_b, None, ALU.add).then_inc(ht_sb, 1)
                dve.wait_ge(h_stored, g * 32 + 32)


def tail(nc, t, out):
    with ExitStack() as ctx:
        def sem(name):
            return ctx.enter_context(nc.semaphore(name))

        def sb(name, n):
            return ctx.enter_context(nc.sbuf_tensor(name, [128, n], F32))[:, :]

        ps = ctx.enter_context(nc.psum_tensor("tail_ps", [128, 8, 512], F32))
        H, K, Vv, R = sb("H", N), sb("K", N), sb("Vv", N), sb("R", N)
        hid = sb("hid", 4 * N)
        A1, A2, A3, A4 = (hid[:, i * N:(i + 1) * N] for i in range(4))
        hT = sb("hT", N)
        ident, wkvr, wo, wr = sb("t_id", 128), sb("wkvr", 384), sb("wo", 128), sb("wr", 128)
        wk_f, wv_f, w1, wg, wd = sb("wk_f", HID), sb("wv_f", 128), sb("w1", HID), sb("wg", 2 * E), sb("wd", 2 * E * CT)
        b1m = sb("b1m", 2)
        bd_diag, bg_bc, gT = sb("bd_diag", 16 * CT), sb("bg_bc", E), sb("gT", 512)
        g1, b1, g2, b2 = sb("g1", 1), sb("b1", 1), sb("g2", 1), sb("b2", 1)
        dec, fst = sb("dec", CT), sb("fst", CT)
        mean, var, rstd = sb("mean", T64), sb("var", T64), sb("rstd", T64)
        lg, gate = sb("lg", T64 * E), sb("gate", T64 * E)
        rank, mx, sm = sb("rank", E), sb("mx", T64), sb("sm", T64)
        kk = sb("kk", 4096)
        rl = sb("rl", 1024)
        prod = sb("prod", 1024)

        h_in, w_in, cleared, stored = sem("h_in"), sem("w_in"), sem("cleared"), sem("stored")
        v = sem("dve_step")
        tp_done, hT_done = sem("tp_done"), sem("hT_done")
        r_ps = sem("r_ps")
        kvr_ps, kvr_sb, sig_sb = sem("kvr_ps"), sem("kvr_sb"), sem("sig_sb")
        wo_ps, wo_sb, r2_ps, r2_sb = sem("wo_ps"), sem("wo_sb"), sem("r2_ps"), sem("r2_sb")
        kf_ps, rl_sb, kk_sb, vf_ps, vf_sb = sem("kf_ps"), sem("rl_sb"), sem("kk_sb"), sem("vf_ps"), sem("vf_sb")
        w1_ps, hid_sb, lg_ps, lg_sb = sem("w1_ps"), sem("hid_sb"), sem("lg_ps"), sem("lg_sb")
        ex_ps, prod_sb, moe_sb = sem("ex_ps"), sem("prod_sb"), sem("moe_sb")
        neg_half, half_in = sb("neg_half", T64), sem("half_in")
        var_in, rstd_in = sem("var_in"), sem("rstd_in")
        ln_in, scan_in = sem("ln_in"), sem("scan_in")
        gate_in, gT_ps, gT_sb, bd_ps, bd_sb = sem("gate_in"), sem("gT_ps"), sem("gT_sb"), sem("bd_ps"), sem("bd_sb")
        logits_in, out_ready, exp_sb = sem("logits_in"), sem("out_ready"), sem("exp_sb")
        NWIN = 1 + 2 * (3 + 4 + 4) + 2 * 4 + 16 + 3
        block = ctx.enter_context(nc.Block())

        def bank(i):
            return ps[:, i, :]

        def tc(ap):
            return ap.rearrange("p (t c) -> p t c", t=T64)

        def ct(ap):
            return ap.rearrange("p (c t) -> p c t", c=CT)

        def over_c(ap):
            return ap.rearrange("p (t o) -> p t o", o=1).to_broadcast([128, T64, CT])

        @block.sync
        def _(sp):
            sp.dma_start(H, t["hs"].rearrange("g r i s f -> (g r i) (s f)")).then_inc(h_in, 16)
            sp.wait_ge(cleared, 1)
            sp.dma_start(ident, t["t_ident"]).then_inc(w_in, 16)
            for t2 in range(2):
                q = slice(64 * t2, 64 * t2 + 64)
                for i, w in enumerate(("Wk", "Wv", "Wr")):
                    c0 = 128 * i + 64 * t2
                    sp.dma_start(wkvr[q, c0:c0 + 64], t["L0_attn_" + w]).then_inc(w_in, 16)
                sp.dma_start(wo[q, q], t["L0_attn_Wo"]).then_inc(w_in, 16)
                sp.dma_start(wr[q, q], t["L0_attn_Wr_ffn"]).then_inc(w_in, 16)
                sp.dma_start(wk_f[q, :], t["L0_attn_Wk_ffn"]).then_inc(w_in, 16)
                sp.dma_start(w1[q, :], t["L0_ffn_W1"]).then_inc(w_in, 16)
                for dst, w in ((g1, "attn_g1"), (b1, "attn_b1"), (g2, "attn_g2"), (b2, "attn_b2")):
                    sp.dma_start(dst[q, :], t["L0_" + w].rearrange("(c o) -> c o", o=1)).then_inc(w_in, 16)
            for m in range(2):
                h = slice(128 * m, 128 * m + 128)
                sp.dma_start(wv_f[:, 64 * m:64 * m + 64], t["L0_attn_Wv_ffn"][h, :]).then_inc(w_in, 16)
                sp.dma_start(wg[:, E * m:E * m + E], t["L0_ffn_Wg"][h, :]).then_inc(w_in, 16)
                sp.dma_start(b1m[:, m:m + 1], t["L0_ffn_b1"][h].rearrange("(c o) -> c o", o=1)).then_inc(w_in, 16)
                sp.dma_start(wd[:, 512 * m:512 * m + 512].rearrange("p (e c) -> p e c", e=E),
                             t["L0_ffn_Wd"][:, h, :].rearrange("e p c -> p e c")).then_inc(w_in, 16)
            for i in range(16):
                sp.dma_start(bd_diag[E * i:E * i + E, CT * i:CT * i + CT], t["L0_ffn_bd"]).then_inc(w_in, 16)
            for dst, w in ((bg_bc, t["L0_ffn_bg"]),
                           (dec, t["L0_attn_spatial_decay"]), (fst, t["L0_attn_spatial_first"])):
                sp.dma_start(dst, w.rearrange("(o n) -> o n", o=1).to_broadcast([128, dst.shape[1]])).then_inc(w_in, 16)
            sp.wait_ge(out_ready, 1)
            sp.dma_start(out.rearrange("b t c -> b (t c)"), A2).then_inc(stored, 16)
            sp.wait_ge(stored, 16)

        @block.vector
        def _(dve):
            n, norms = [0], [0]

            def step(ins):
                n[0] += 1
                ins.then_inc(v, 1)
                dve.wait_ge(v, n[0])

            def layer_norm(src, dst, tmp):
                step(nc.vector.tensor_reduce(mean, tc(src), AX.X, ALU.add))
                step(nc.vector.tensor_scalar(mean, mean, 1.0 / CT, None, ALU.mult))
                step(nc.vector.tensor_tensor(tc(dst), tc(src), over_c(mean), ALU.subtract))
                step(nc.vector.tensor_tensor(tmp, dst, dst, ALU.mult))
                step(nc.vector.tensor_reduce(var, tc(tmp), AX.X, ALU.add))
                step(nc.vector.tensor_scalar(var, var, 1.0 / CT, 1e-5, ALU.mult, ALU.add))
                norms[0] += 1
                nc.vector.engine_nop().then_inc(var_in, 1)
                dve.wait_ge(rstd_in, norms[0])
                step(nc.vector.tensor_tensor(tc(dst), tc(dst), over_c(rstd), ALU.mult))

            def turned(i, gain=None, bias=None):
                for k in range(8):
                    dve.wait_ge(tp_done, 8 * i + k + 1)
                    o = hT[:, 512 * k:512 * k + 512]
                    if gain is None:
                        nc.vector.tensor_copy(o, bank(k)).then_inc(hT_done, 1)
                    else:
                        nc.vector.tensor_scalar(o, bank(k), gain, bias, ALU.mult, ALU.add).then_inc(hT_done, 1)

            nc.vector.memset(wkvr, 0.0)
            nc.vector.memset(bd_diag, 0.0)
            nc.vector.memset(wo, 0.0)
            nc.vector.memset(wr, 0.0).then_inc(cleared, 1)
            for e in range(E):
                m = nc.vector.memset(rank[:, e:e + 1], float(E - e))
            step(m)
            dve.wait_ge(w_in, 16 * NWIN)
            step(nc.vector.tensor_scalar(dec, dec, 1.0 / T64, None, ALU.mult))
            step(nc.vector.tensor_scalar(fst, fst, 1.0 / T64, None, ALU.mult))
            dve.wait_ge(h_in, 16)
            layer_norm(H, A1, A2)
            nc.vector.engine_nop().then_inc(ln_in, 1)
            turned(0, g1, b1)
            for tp in range(TP):
                dve.wait_ge(kvr_ps, tp + 1)
                src = bank(tp % 4)[:, 0:256].rearrange("p (k t c) -> p k c t", k=2, t=2)
                nc.vector.tensor_copy(ct(K)[:, :, 2 * tp:2 * tp + 2], src[:, 0])
                nc.vector.tensor_copy(ct(Vv)[:, :, 2 * tp:2 * tp + 2], src[:, 1]).then_inc(kvr_sb, 1)
            dve.wait_ge(kvr_sb, TP)
            late, early = slice(1, T64), slice(0, T64 - 1)
            tt = nc.vector.tensor_tensor
            per_c = lambda ap, n_: ap.rearrange("p (c o) -> p c o", o=1).to_broadcast([128, CT, n_])
            step(nc.vector.tensor_copy(ct(A1), per_c(dec, T64)))
            step(nc.vector.memset(ct(A1)[:, :, 0:1], NEG))
            step(nc.vector.tensor_tensor_scan(A2, A1, K, NEG, ALU.add, ALU.max))
            step(tt(A3, A1, A2, ALU.subtract))
            step(tt(ct(A3)[:, :, late], ct(A3)[:, :, late], ct(A2)[:, :, early], ALU.add))
            step(tt(ct(A4), ct(K), per_c(fst, T64), ALU.add))
            step(nc.vector.tensor_copy(A1, A4))
            step(tt(ct(A1)[:, :, late], ct(A4)[:, :, late], ct(A2)[:, :, early], ALU.max))
            step(tt(A4, A4, A1, ALU.subtract))
            step(tt(ct(A1)[:, :, late], ct(A2)[:, :, early], ct(A1)[:, :, late], ALU.subtract))
            step(nc.vector.memset(ct(A1)[:, :, 0:1], NEG))
            step(tt(K, K, A2, ALU.subtract))
            nc.vector.engine_nop().then_inc(scan_in, 1)
            dve.wait_ge(exp_sb, 4)
            dve.wait_ge(sig_sb, TP)
            step(tt(hT, K, Vv, ALU.mult))
            step(nc.vector.tensor_tensor_scan(A2, A3, hT, 0.0, ALU.mult, ALU.add))
            step(nc.vector.tensor_tensor_scan(hT, A3, K, 0.0, ALU.mult, ALU.add))
            step(tt(A3, A4, Vv, ALU.mult))
            step(tt(ct(A2)[:, :, early], ct(A1)[:, :, late], ct(A2)[:, :, early], ALU.mult))
            step(tt(ct(A3)[:, :, late], ct(A3)[:, :, late], ct(A2)[:, :, early], ALU.add))
            step(tt(ct(hT)[:, :, early], ct(A1)[:, :, late], ct(hT)[:, :, early], ALU.mult))
            step(tt(ct(A4)[:, :, late], ct(A4)[:, :, late], ct(hT)[:, :, early], ALU.add))
            step(nc.vector.reciprocal(A4, A4))
            step(tt(A3, A3, A4, ALU.mult))
            step(tt(tc(A1), tc(R), ct(A3).rearrange("p c t -> p t c"), ALU.mult))
            nc.vector.engine_nop().then_inc(ln_in, 1)
            turned(1)
            for k in range(8):
                dve.wait_ge(wo_ps, k + 1)
                c = slice(512 * k, 512 * k + 512)
                tt(A2[:, c], H[:, c], bank(k), ALU.add).then_inc(wo_sb, 1)
            dve.wait_ge(wo_sb, 8)
            layer_norm(A2, A1, A3)
            nc.vector.engine_nop().then_inc(ln_in, 1)
            turned(2, g2, b2)
            for f in range(32):
                i = f // 4
                dve.wait_ge(rl_sb, f + 1)
                if i >= 2 and f % 4 == 0:
                    dve.wait_ge(vf_ps, i - 1)
                r = rl[:, f % 2 * 512:f % 2 * 512 + 512]
                tt(kk[:, f % 8 * 512:f % 8 * 512 + 512], r, r, ALU.mult).then_inc(kk_sb, 1)
                if f % 4 == 3:
                    dve.wait_ge(vf_ps, i + 1)
                    c = slice(512 * i, 512 * i + 512)
                    tt(A3[:, c], R[:, c], bank(6 + i % 2), ALU.mult).then_inc(vf_sb, 1)
            dve.wait_ge(vf_sb, 8)
            step(tt(A2, A2, A3, ALU.add))
            step(tt(H, H, A2, ALU.add))
            layer_norm(H, K, Vv)
            nc.vector.engine_nop().then_inc(ln_in, 1)
            turned(3)
            for k in range(8):
                dve.wait_ge(lg_ps, k + 1)
                c = slice(64 * k, 64 * k + 64)
                tt(lg[:, c].rearrange("p (t e) -> p t e", e=E), bank(6 + k % 2)[:, 0:64].rearrange("p (t e) -> p t e", e=E),
                   bg_bc.rearrange("p (o e) -> p o e", o=1).to_broadcast([128, 8, E]), ALU.add).then_inc(lg_sb, 1)
            dve.wait_ge(lg_sb, 8)
            te = lambda ap: ap.rearrange("p (t e) -> p t e", e=E)
            over_e = lambda ap: ap.rearrange("p (t o) -> p t o", o=1).to_broadcast([128, T64, E])
            step(nc.vector.tensor_reduce(mx, te(lg), AX.X, ALU.max))
            step(tt(te(lg), te(lg), over_e(mx), ALU.subtract))
            nc.vector.engine_nop().then_inc(logits_in, 1)
            dve.wait_ge(exp_sb, 5)
            step(nc.vector.tensor_reduce(sm, te(lg), AX.X, ALU.add))
            step(nc.vector.reciprocal(sm, sm))
            step(tt(te(lg), te(lg), over_e(sm), ALU.mult))
            step(nc.vector.tensor_reduce(mx, te(lg), AX.X, ALU.max))
            step(tt(te(gate), te(lg), over_e(mx), ALU.is_equal))
            step(tt(te(gate), te(gate), rank.rearrange("p (o e) -> p o e", o=1).to_broadcast([128, T64, E]), ALU.mult))
            step(nc.vector.tensor_reduce(sm, te(gate), AX.X, ALU.max))
            step(tt(te(gate), te(gate), over_e(sm), ALU.is_equal))
            step(tt(te(gate), te(gate), over_e(mx), ALU.mult))
            nc.vector.engine_nop().then_inc(gate_in, 1)
            dve.wait_ge(gT_ps, 1)
            nc.vector.tensor_copy(gT, bank(4)).then_inc(gT_sb, 1)
            for k in range(8):
                dve.wait_ge(bd_ps, k + 1)
                c = slice(512 * k, 512 * k + 512)
                tt(K[:, c], K[:, c], bank(k), ALU.add).then_inc(bd_sb, 1)
            dve.wait_ge(bd_sb, 8)
            for i in range(T64):
                dve.wait_ge(ex_ps, i + 1)
                p = prod[:, i % 2 * 512:i % 2 * 512 + 512]
                pe_ = p.rearrange("p (e c) -> p e c", e=E)
                tt(pe_, bank(i % 4).rearrange("p (e c) -> p e c", e=E),
                   gate[:, E * i:E * i + E].rearrange("p (e o) -> p e o", o=1).to_broadcast([128, E, CT]),
                   ALU.mult).then_inc(prod_sb, 1)
                dve.wait_ge(prod_sb, i + 1)
                nc.vector.tensor_reduce(Vv[:, CT * i:CT * i + CT], p.rearrange("p (e c) -> p c e", e=E),
                                        AX.X, ALU.add).then_inc(moe_sb, 1)
            dve.wait_ge(moe_sb, T64)
            step(tt(K, K, Vv, ALU.add))
            layer_norm(K, A2, A3)
            nc.vector.engine_nop().then_inc(out_ready, 1)

        @block.tensor
        def _(pe):
            mm = nc.tensor.matmul

            def turn(i, src):
                pe.wait_ge(ln_in, i + 1)
                for k in range(8):
                    for j in range(4):
                        c0 = 512 * k + 128 * j
                        m = nc.tensor.transpose(bank(k)[:, 128 * j:128 * j + 128], src[:, c0:c0 + 128], ident)
                    m.then_inc(tp_done, 1)

            def pair(tp):
                return hT[:, 128 * tp:128 * tp + 128]

            pe.wait_ge(w_in, 16 * NWIN)
            turn(0, A1)
            pe.wait_ge(hT_done, 8)
            for tp in range(TP):
                if tp >= 4:
                    pe.wait_ge(kvr_sb, tp - 3)
                    pe.wait_ge(sig_sb, tp - 3)
                mm(bank(tp % 4)[:, 0:256], pair(tp), wkvr[:, 0:256], start=True, stop=True).then_inc(kvr_ps, 1)
                mm(bank(4 + tp % 4)[:, 0:128], pair(tp), wkvr[:, 256:384], start=True, stop=True).then_inc(r_ps, 1)
            pe.wait_ge(sig_sb, TP)
            pe.wait_ge(kvr_sb, TP)
            turn(1, A1)
            for k in range(8):
                pe.wait_ge(hT_done, 8 + k + 1)
                for j in range(4):
                    m = mm(bank(k)[:, 128 * j:128 * j + 128], pair(4 * k + j), wo, start=True, stop=True)
                m.then_inc(wo_ps, 1)
            pe.wait_ge(wo_sb, 8)
            turn(2, A1)
            pe.wait_ge(hT_done, 24)
            for k in range(8):
                for j in range(4):
                    m = mm(bank(k)[:, 128 * j:128 * j + 128], pair(4 * k + j), wr, start=True, stop=True)
                m.then_inc(r2_ps, 1)
            pe.wait_ge(r2_sb, 8)

            def hidden(i, w, filled, emptied):
                for k in range(4):
                    f = 4 * i + k
                    t2, m = divmod(k, 2)
                    q = slice(64 * t2, 64 * t2 + 64)
                    if f >= 4:
                        pe.wait_ge(emptied, f - 3)
                    mm(bank(f % 4), w[q, 128 * m:128 * m + 128], hT[q, 512 * i:512 * i + 512],
                       start=True, stop=True).then_inc(filled, 1)

            hidden(0, wk_f, kf_ps, rl_sb)
            for i in range(8):
                if i < 7:
                    hidden(i + 1, wk_f, kf_ps, rl_sb)
                pe.wait_ge(kk_sb, 4 * i + 4)
                if i >= 2:
                    pe.wait_ge(vf_sb, i - 1)
                for j in range(8):
                    for m in range(2):
                        c0 = (4 * (i % 2) + 2 * (j % 2) + m) * 512 + 128 * (j // 2)
                        ins = mm(bank(6 + i % 2)[:, CT * j:CT * j + CT], kk[:, c0:c0 + 128],
                                 wv_f[:, CT * m:CT * m + CT], start=m == 0, stop=m == 1)
                ins.then_inc(vf_ps, 1)
            turn(3, K)
            pe.wait_ge(hT_done, 32)
            hidden(0, w1, w1_ps, hid_sb)
            for i in range(8):
                if i < 7:
                    hidden(i + 1, w1, w1_ps, hid_sb)
                pe.wait_ge(hid_sb, 4 * i + 4)
                if i >= 2:
                    pe.wait_ge(lg_sb, i - 1)
                for j in range(8):
                    for m in range(2):
                        c0 = m * 2 * N + (8 * i + j) * 128
                        ins = mm(bank(6 + i % 2)[:, E * j:E * j + E], hid[:, c0:c0 + 128],
                                 wg[:, E * m:E * m + E], start=m == 0, stop=m == 1)
                ins.then_inc(lg_ps, 1)
            pe.wait_ge(gate_in, 1)
            for k in range(4):
                m = nc.tensor.transpose(bank(4)[:, 128 * k:128 * k + 128], gate[:, 128 * k:128 * k + 128], ident)
            m.then_inc(gT_ps, 1)
            pe.wait_ge(gT_sb, 1)
            for k in range(8):
                mm(bank(k), gT[:, 128 * (k // 2):128 * (k // 2) + 128], bd_diag[:, 512 * (k % 2):512 * (k % 2) + 512],
                   start=True, stop=True).then_inc(bd_ps, 1)
            pe.wait_ge(bd_sb, 8)
            for i in range(T64):
                if i >= 4:
                    pe.wait_ge(prod_sb, i - 3)
                for m in range(2):
                    c0 = m * 2 * N + i * 128
                    ins = mm(bank(i % 4), hid[:, c0:c0 + 128], wd[:, 512 * m:512 * m + 512],
                             start=m == 0, stop=m == 1)
                ins.then_inc(ex_ps, 1)

        @block.gpsimd
        def _(pool):
            nc.gpsimd.memset(neg_half, -0.5).then_inc(half_in, 1)
            pool.wait_ge(half_in, 1)
            for i in range(4):
                pool.wait_ge(var_in, i + 1)
                nc.gpsimd.tensor_tensor(rstd, var, neg_half, ALU.pow).then_inc(rstd_in, 1)

        @block.scalar
        def _(act):
            for tp in range(TP):
                act.wait_ge(r_ps, tp + 1)
                nc.scalar.activation(R[:, 128 * tp:128 * tp + 128], bank(4 + tp % 4)[:, 0:128],
                                     ACT.Sigmoid).then_inc(sig_sb, 1)
            act.wait_ge(scan_in, 1)
            for ap in (A3, A1, A4, K):
                nc.scalar.activation(ap, ap, ACT.Exp).then_inc(exp_sb, 1)
            for k in range(8):
                act.wait_ge(r2_ps, k + 1)
                nc.scalar.activation(R[:, 512 * k:512 * k + 512], bank(k), ACT.Sigmoid).then_inc(r2_sb, 1)
            for f in range(32):
                act.wait_ge(kf_ps, f + 1)
                if f >= 2:
                    act.wait_ge(kk_sb, f - 1)
                nc.scalar.activation(rl[:, f % 2 * 512:f % 2 * 512 + 512], bank(f % 4), ACT.Relu).then_inc(rl_sb, 1)
            act.wait_ge(w_in, 16 * NWIN)
            for f in range(32):
                i, t2, m = f // 4, f // 2 % 2, f % 2
                act.wait_ge(w1_ps, f + 1)
                c0 = m * 2 * N + i * 1024
                dst = hid[:, c0:c0 + 1024].rearrange("p (j t b) -> p t j b", j=4, t=2)[:, t2]
                nc.scalar.activation(dst, bank(f % 4).rearrange("p (j b) -> p j b", j=4), ACT.Gelu,
                                     bias=b1m[:, m:m + 1]).then_inc(hid_sb, 1)
            act.wait_ge(logits_in, 1)
            nc.scalar.activation(lg, lg, ACT.Exp).then_inc(exp_sb, 1)


def build(nc, t, out):
    tokenizer(nc, t)
    tail(nc, t, out)


def laid_out(inputs):
    a = {k: np.asarray(v) for k, v in inputs.items()}
    d = {"x": a["x"].reshape(GROUPS_ALL, G, J, HG, HW, 3).transpose(0, 1, 2, 5, 3, 4).reshape(GROUPS_ALL, G, 12, PIX)}
    d["sw"] = np.stack([a[f"L0_tok_sw{l}"].reshape(CH, CH, 4, 5, 10, 2).transpose(4, 3, 0, 2, 5, 1).reshape(10, 5, CH, 8, CH)
                        for l in range(LAYERS)])
    d["cw"] = np.stack([a[f"L0_tok_cw{l}"].T for l in range(LAYERS)])
    d["cb"] = np.stack([a[f"L0_tok_cb{l}"].reshape(CH, 1) for l in range(LAYERS)])
    for k, v in a.items():
        if k.startswith("L0_tok_fc") or k.startswith("L0_attn") or k.startswith("L0_ffn"):
            d[k] = v.reshape(-1, 1) if v.ndim == 1 and k.startswith("L0_tok") else v
    return {k: np.ascontiguousarray(v) for k, v in d.items()}


GROUPS_ALL = GROUPS


def kernel(**inputs):
    import concourse.bacc as bacc
    from concourse.bass_utils import run_bass_kernel_spmd

    nc = bacc.Bacc("TRN2", target_bir_lowering=False, num_devices=1)
    arrays = laid_out(inputs)
    arrays.update({k: np.ascontiguousarray(v.astype(np.float32)) for k, v in dft_tables().items()})
    t = {k: nc.dram_tensor(k, v.shape, F32, kind="ExternalInput").ap() for k, v in arrays.items()}
    t["hs"] = nc.dram_tensor("hs", (GROUPS, PAIRS, 2, 16, 256), F32, kind="Internal").ap()
    out = nc.dram_tensor("out", (B, HW, HW), F32, kind="ExternalOutput").ap()
    build(nc, t, out)
    r = run_bass_kernel_spmd(nc, [arrays], core_ids=[0])
    return r.results[0]["out"]
```

```python
from contextlib import ExitStack

import numpy as np

import concourse.bass as bass
from concourse import mybir

F32 = mybir.dt.float32
ALU = mybir.AluOpType
ACT = mybir.ActivationFunctionType
AX = mybir.AxisListType

B, HW, CH, MODES, LAYERS = 128, 64, 32, 20, 4
G = 16
GROUPS = B // G
PAIRS, QUADS = G // 2, G // 4
J = 4
OCTS = PAIRS // J
OCT = 2 * HW * HW
KR = 2 * MODES
HID, E = 256, 8
TP = HW // 2
T64, CT = HW, HW
N = HW * HW
NW = 96
NEG = -1e38
FC = 256 + 191


def dft_tables():
    k, n = np.arange(MODES), np.arange(HW)
    ang = 2 * np.pi * np.outer(n, k) / HW
    cos, sin = np.cos(ang) / 8, np.sin(ang) / 8
    over_w = np.zeros((J, HW // 2, 2, J, 2, MODES))
    over_h = np.zeros((2, HW, 80 + NW))
    h6 = over_h[..., :160].reshape(2, HW, 2, 2, 2, MODES)
    back_h = np.zeros((128, 2, HW))
    rows = back_h[:2 * KR].reshape(2, 4, 2, 5, 2, HW)
    back_w = np.zeros((128, 2, HW))
    twice = np.where(k == 0, 1.0, 2.0)[:, None]
    for i in range(2):
        h6[i, :, 0, i, 0], h6[i, :, 0, i, 1] = cos, -sin
        h6[i, :, 1, i, 0], h6[i, :, 1, i, 1] = sin, cos
        rows[0, :, i, :, i], rows[1, :, i, :, i] = cos.T.reshape(4, 5, HW), -sin.T.reshape(4, 5, HW)
        back_w[64 * i:64 * i + KR, i] = np.concatenate([twice * cos.T, -twice * sin.T])
    for i in range(J):
        for h in range(2):
            over_w[i, :, h, i, 0], over_w[i, :, h, i, 1] = cos[32 * h:32 * h + 32], -sin[32 * h:32 * h + 32]
    return {"t_over_w": over_w.reshape(128, 2 * J * KR), "t_over_h": over_h.reshape(128, 80 + NW), "t_back_h": back_h.reshape(128, 128),
            "t_back_w": back_w.reshape(128, 128), "t_ident": np.eye(128),
            "t_fold": np.tile(np.eye(64), (2, 1)),
            "t_quads": np.repeat(np.eye(4), CH, axis=0)}


def tokenizer(nc, t):
    with ExitStack() as ctx:
        def sem(name):
            return ctx.enter_context(nc.semaphore(name))

        MODE_WORDS = CH // 2 * KR * G + 2 * 5 * MODES * CH
        WORDS = 53208 - MODE_WORDS
        arena = ctx.enter_context(nc.sbuf_tensor("arena", [128, WORDS], F32))
        with nc.sbuf_tensor("modes", [128, MODE_WORDS], F32) as modes:
            pass
        parts = ctx.enter_context(nc.sbuf_tensor("parts", [128, MODE_WORDS], F32))
        ps = ctx.enter_context(nc.psum_tensor("ps", [128, 8, 512], F32))
        top = [0]

        def take(n):
            top[0] += n
            assert top[0] <= WORDS, top
            return arena[:, top[0] - n:top[0]]

        over_w, over_h, back_h, back_w = take(2 * J * KR), take(80 + NW), take(128), take(128)
        cwb = take(129)
        cw, cb = cwb[:, 0:128], cwb[:, 128:129]
        biases, fold = take(3), take(64)
        fc0_b, fc1_b, fc2_b = (biases[:, i:i + 1] for i in range(3))
        x = take(OCTS * OCT)
        TW = 4096
        T = [take(TW), take(TW)]
        F2 = T[0]
        gel = T[0][:, 0:2048]
        ht = T[0][:, 2048:2560]
        xin = T[1]
        Xt = take(3 * 1280 + 256)
        Z = arena[:, top[0] - 8192:top[0]]
        VR = 64 + KR
        VROWS = VR * CH
        Y = modes[:, 0:CH // 2 * KR * G]
        V = [Y[:, i * VROWS:(i + 1) * VROWS] for i in range(2)]
        fc0_w = Y[:, 9216:9216 + 128]
        SW = 5 * 8 * CH
        stage = take(SW)
        stage_last = Y[:, 2 * VROWS:2 * VROWS + SW]
        SF = 5 * MODES * CH
        S = modes[:, MODE_WORDS - 2 * SF:MODE_WORDS - SF]
        Sn = modes[:, MODE_WORDS - SF:MODE_WORDS]
        W = [take(8 * 128) for a in range(5)] + [Y[:, a * 1024:(a + 1) * 1024] for a in range(5)]
        fc_raw = S[:, 0:FC]
        fc_hi, fc1_lo, fc2_w = (parts[:, MODE_WORDS - SF + i:MODE_WORDS - SF + j]
                                for i, j in ((0, FC), (FC, FC + 256), (FC + 256, FC + 447)))
        xh, xl, gh, gl = (parts[:, 2048 * i:2048 * i + 2048] for i in range(4))
        acc = Y[:, 8192:8192 + 512]
        SIDE = 2 * VROWS + SW
        ch, cl = ([parts[:, i + 512 * k:i + 512 * k + 512] for i in (SIDE, SIDE + 1024, 2 * VROWS)] for k in range(2))
        cw_hi, cw_lo = parts[:, SIDE + 2048:SIDE + 2176], parts[:, SIDE + 2176:SIDE + 2304]
        quads = take(4)
        gate_in, gate_out = take(1), take(1)

        NCONST = 7
        consts = sem("consts")
        zeroed, gated = sem("zeroed"), sem("gated")
        x_ready, tp_ps, t_sb, y_ps, y_sb = sem("x_ready"), sem("tp_ps"), sem("t_sb"), sem("y_ps"), sem("y_sb")
        f2_ps, f2_sb, xt_sb = sem("f2_ps"), sem("f2_sb"), sem("xt_sb")
        staged, w_spread = [sem(f"staged{i}") for i in range(3)], sem("w_spread")
        mix_ps, s_sb, sn_sb = sem("mix_ps"), sem("s_sb"), sem("sn_sb")
        v_loaded = [sem(f"v_loaded{i}") for i in range(4)]
        z_ps, z_sb, o_ps, layer_w = sem("z_ps"), sem("z_sb"), sem("o_ps"), sem("layer_w")
        xin_loaded = [sem("xin_loaded0"), sem("xin_loaded1")]
        fc0_loaded, fc0_ps, fc1_ps, g_sb, fc2_ps = sem("fc0_loaded"), sem("fc0_ps"), sem("fc1_ps"), sem("g_sb"), sem("fc2_ps")
        fc_loaded, fc_cut, fc_split, acc_sb, fold_ps = (sem(n) for n in ("fc_loaded", "fc_cut", "fc_split", "acc_sb",
                                                                       "fold_ps"))
        cwh_sb, cw_sb, ch_sb, cl_sb, mixed = sem("cwh_sb"), sem("cw_sb"), sem("ch_sb"), sem("cl_sb"), sem("mixed")
        xh_sb, xl_sb, gh_sb, gl_sb = sem("xh_sb"), sem("xl_sb"), sem("gh_sb"), sem("gl_sb")
        ht_sb, h_stored = sem("ht_sb"), sem("h_stored")

        block = ctx.enter_context(nc.Block())

        def bank(i):
            return ps[:, i, :]

        Y_RING, F2_RING, S_RING, Z_RING = (2, 3, 6, 7), (4, 5, 1, 7), (0, 2, 3, 6), (2, 3, 1)
        OUT_RING = (4, 5, 6, 7, 0)

        FC1_RING, ACC = (6, 7, 4, 5), (2, 0)

        def slot(ring, n):
            return ring[:, n % 4 * 512:n % 4 * 512 + 512]

        def r(ap):
            return ap.bitcast(mybir.dt.float32r)

        def bank8(i):
            return ps[:, i, :].rearrange("p (h w) -> p h w", h=8)

        def xcols(n):
            o, i, k = n // 16, n // 8 % 2, n % 8
            return x[:, o * OCT:(o + 1) * OCT].rearrange("p (h i w) -> p i h w", h=HW, i=2)[:, i, 8 * k:8 * k + 8, :]

        SP_V = 5

        def spread(n, first=None):
            tt, a = divmod(n, 5)
            Q = 4 if tt < 2 else 2
            dst = W[n % 10].rearrange("p (m q f) -> p m q f", m=8, q=4)[:, :, 0:Q]
            src = (stage, stage, stage_last)[tt if first is None else 2][:, a * 256:(a + 1) * 256].rearrange("p (m o f) -> p m o f", m=8, o=1)
            own = quads[:, 0:Q].rearrange("p (o q u) -> p o q u", o=1, u=1)
            nc.gpsimd.tensor_tensor(dst, src.to_broadcast([128, 8, Q, CH]), own.to_broadcast([128, 8, Q, CH]),
                                    ALU.mult).then_inc(w_spread, 1)

        def load_v(eng, it, first, gate):
            eng.wait_ge(s_sb, it * 15 + 15)
            eng.wait_ge(sn_sb, it * 15 + 15)
            gate(it, 0)
            for qd in range(QUADS):
                if qd >= 2:
                    eng.wait_ge(z_ps, it * 32 + 8 * (qd - 1))
                    gate(it, qd - 1)
                for n in range(SP_V) if first else range(SP_V, 8):
                    i, kr, rr = n // 4, n // 2 % 2, n % 2
                    p0 = 8 * (kr ^ rr) + 4 * (qd % 2) + 2 * (qd // 2) + i
                    src = (Sn if kr and rr else S)[p0:p0 + 113:16, :].rearrange("p (a f) -> p a f", a=5)
                    c0 = (i * 64 + rr * MODES) * CH
                    eng.dma_start(V[qd % 2][KR * kr:KR * kr + KR, c0:c0 + MODES * CH],
                                  src).then_inc(v_loaded[2 * (1 - first) + qd % 2], 16)

        @block.gpsimd
        def _(pool):
            def gate(it, i):
                pool.wait_ge(gated, it * 3 + i + 1)
                nc.gpsimd.tensor_tensor(gate_out, gate_in, gate_in, ALU.add).then_inc(gated, 1)

            nc.gpsimd.memset(gate_in, 0.0).then_inc(gated, 1)
            pool.wait_ge(gated, 1)
            pool.wait_ge(zeroed, 1)
            pool.wait_ge(consts, 16 * NCONST)
            pool.wait_ge(staged[0], 16)
            for n in range(5):
                spread(n, True)
            with pool.Fori(0, GROUPS) as g:
                with pool.Fori(0, LAYERS) as l:
                    it = g * LAYERS + l
                    pool.wait_ge(staged[1], it * 16 + 16)
                    for n in range(5, 10):
                        pool.wait_ge(f2_ps, it * 12 + (9, 9, 10, 10, 10)[n - 5])
                        spread(n)
                    pool.wait_ge(staged[2], it * 16 + 16)
                    for n in range(10, 15):
                        pool.wait_ge(mix_ps, it * 15 + n - 9)
                        spread(n)
                    load_v(pool, it, False, gate)
                    pool.wait_ge(staged[0], it * 16 + 32)
                    for n in range(5):
                        spread(n)
                for nb in range(2 * G):
                    if nb >= 4:
                        pool.wait_ge(fc1_ps, g * 64 + 2 * (nb - 3))
                    pool.wait_ge(xh_sb, g * 32 + nb + 1)
                    nc.gpsimd.tensor_tensor(r(slot(xl, nb)), x[:, 512 * nb:512 * nb + 512], slot(xh, nb),
                                            ALU.subtract).then_inc(xl_sb, 1)

        @block.sync
        def _(sp):
            for dst, name in ((biases, "fc_b"), (over_w, "t_over_w"), (quads, "t_quads"), (over_h, "t_over_h"),
                              (back_h, "t_back_h"), (back_w, "t_back_w"), (fold, "t_fold")):
                sp.dma_start(dst, t[name]).then_inc(consts, 16)
            sp.dma_start(stage_last, t["sw"][0, 0:128]).then_inc(staged[0], 16)
            sp.dma_start(stage, t["sw"][0, 128:256]).then_inc(staged[1], 16)
            with sp.Fori(0, GROUPS) as g:
                sp.dma_start(fc0_w, t["fc0_w"]).then_inc(fc0_loaded, 16)
                sp.wait_ge(zeroed, 1)
                for im in range(G):
                    if im >= 2:
                        sp.wait_ge(fc0_ps, g * 32 + 2 * (im - 1))
                    sp.dma_start(xin[0:12, im % 2 * 1024:(im % 2 + 1) * 1024],
                                 t["x"][g, im // 8, im // 4 % 2, im % 4]).then_inc(xin_loaded[im % 2], 16)
                with sp.Fori(0, LAYERS) as l:
                    it = g * LAYERS + l
                    sp.wait_ge(x_ready, g * 160 + l * 32 + 32)
                    sp.dma_start(cwb, t["cwb"][l]).then_inc(layer_w, 16)
                    sp.wait_ge(f2_ps, it * 12 + 12)
                    sp.dma_start(stage_last[0:64, :], t["sw"][l, 256:320]).then_inc(staged[2], 16)
                    load_v(sp, it, True, lambda it, i: None)
                    sp.wait_ge(w_spread, it * 15 + 15)
                    sp.dma_start(stage, t["sw"][l + 1, 0:128]).then_inc(staged[0], 16)
                    sp.wait_ge(w_spread, it * 15 + 20)
                    sp.dma_start(stage, t["sw"][l + 1, 128:256]).then_inc(staged[1], 16)
                for i, count in enumerate((SP_V, 8 - SP_V)):
                    for k in range(2):
                        sp.wait_ge(v_loaded[2 * i + k], g * 32 * LAYERS * count + 32 * LAYERS * count)
                sp.dma_start(fc_raw, t["fc_w"]).then_inc(fc_loaded, 16)
                sp.wait_ge(ht_sb, g + 1)
                for i in range(2):
                    sp.dma_start(t["hs"][g, :, i], ht[:, 256 * i:256 * i + 256]).then_inc(h_stored, 16)
            sp.wait_ge(h_stored, GROUPS * 32)
            for i in range(2):
                sp.wait_ge(staged[i], 16 * (GROUPS * LAYERS + 1))

        @block.tensor
        def _(pe):
            mm = nc.tensor.matmul
            with pe.Fori(0, GROUPS) as g:
                pe.wait_ge(fc0_loaded, g * 16 + 16)
                for n in range(2 * G):
                    im, b = divmod(n, 2)
                    if b == 0:
                        pe.wait_ge(xin_loaded[im % 2], g * 128 + 16 * (im // 2 + 1))
                    if n >= 4:
                        pe.wait_ge(x_ready, g * 160 + n - 3)
                    c0 = im % 2 * 1024 + b * 512
                    mm(bank(4 + n % 4), fc0_w, xin[:, c0:c0 + 512],
                       start=True, stop=True).then_inc(fc0_ps, 1)

                with pe.Fori(0, LAYERS) as l:
                    it = g * LAYERS + l

                    pe.wait_ge(consts, 16 * NCONST)
                    for u in range(4):
                        pe.wait_ge(t_sb, g * (16 * LAYERS + 4) + l * 16 + 4 * (u + 1))
                        for k in range(8):
                            n = 8 * u + k
                            if n == 2:
                                pe.wait_ge(x_ready, g * 160 + l * 32 + 32)
                            if n >= 4:
                                pe.wait_ge(y_sb, it * 32 + n - 3)
                            for c in range(2):
                                for wh in range(2):
                                    c0 = wh * 2048 + (2 * k + c) * 128
                                    m = mm(bank(Y_RING[n % 4])[:, 160 * c:160 * c + 160], T[u % 2][:, c0:c0 + 128],
                                           over_w[:, 160 * wh:160 * wh + 160], start=wh == 0, stop=wh == 1)
                            m.then_inc(y_ps, 1)

                    for n in range(12):
                        tt, k = divmod(n, 4)
                        M, w = (128, NW) if tt < 2 else (64, 80)
                        if tt == 0:
                            pe.wait_ge(y_sb, it * 32 + 24 + 2 * (k + 1))
                        if n >= 4:
                            pe.wait_ge(f2_sb, it * 12 + n - 3)
                        for c in range(4):
                            for ri in range(2):
                                c0 = ((4 * k + c) * 2 + ri) * MODES * G + tt * 128
                                m = mm(bank(F2_RING[n % 4])[0:M, NW * c:NW * c + w], Y[:, c0:c0 + M],
                                       over_h[:, 80 * ri:80 * ri + w], start=ri == 0, stop=ri == 1)
                        m.then_inc(f2_ps, 1)

                    for n in range(15):
                        tt, a = divmod(n, 5)
                        P = 128 if tt < 2 else 64
                        pe.wait_ge(xt_sb, it * 3 + tt + 1)
                        pe.wait_ge(w_spread, it * 15 + n + 1)
                        if n >= 4:
                            pe.wait_ge(s_sb, it * 15 + n - 3)
                        for b in range(4):
                            for k2 in range(2):
                                c0 = tt * 1280 + (5 * b + a) * 64
                                lhsT = Xt[:, c0 + 32 * k2:c0 + 32 * k2 + 32]
                                o = bank(S_RING[n % 4])[32 * b:32 * b + 32, 0:2 * P].rearrange("p (q k o) -> p q k o", k=2, o=CH)
                                c1 = (2 * b + k2) * 128
                                m = mm(o[:, :, k2], lhsT, W[n % 10][:, c1:c1 + P], start=True, stop=True)
                        m.then_inc(mix_ps, 1)

                    def back_over_h(qd):
                        for i, count in enumerate((SP_V, 8 - SP_V)):
                            pe.wait_ge(v_loaded[2 * i + qd % 2], it * 32 * count + 16 * count * (qd // 2 + 1))
                        for k in range(8):
                            n = 8 * qd + k
                            if n >= 3:
                                pe.wait_ge(z_sb, it * 32 + n - 2)
                            for c in range(4):
                                m = mm(bank(Z_RING[n % 3])[0:VR, 128 * c:128 * c + 128],
                                       V[qd % 2][:, 4 * k + c:VROWS:CH], back_h, start=True, stop=True)
                            m.then_inc(z_ps, 1)

                    def channels(n):
                        o = bank(OUT_RING[n % 5])
                        pe.wait_ge(ch_sb, it * 32 + n + 1)
                        mm(o, r(cw_hi), r(ch[n % 3]), start=True, stop=False)
                        mm(o, r(cw_lo), r(ch[n % 3]), start=False, stop=False)
                        pe.wait_ge(cl_sb, it * 32 + n + 1)
                        mm(o, r(cw_hi), r(cl[n % 3]), start=False, stop=False).then_inc(mixed, 1)

                    def finish(o):
                        pe.wait_ge(z_sb, it * 32 + 16 * (o + 1))
                        for k in range(16):
                            n = 16 * o + k
                            if k >= 5:
                                pe.wait_ge(x_ready, g * 160 + (l + 1) * 32 + n - 4)
                                channels(n)
                            for h in range(4):
                                z0 = (4 * k + h) * 128
                                m = mm(bank(OUT_RING[n % 5])[:, 128 * h:128 * h + 128], Z[0:VR, z0:z0 + 128],
                                       back_w[0:VR, :], start=False, stop=h == 3)
                            m.then_inc(o_ps, 1)

                    pe.wait_ge(cw_sb, it + 1)
                    for n in range(5):
                        if n == 2:
                            pe.wait_ge(s_sb, it * 15 + 15)
                        channels(n)
                    back_over_h(0)
                    back_over_h(1)
                    finish(0)
                    back_over_h(2)
                    back_over_h(3)
                    for n in range(16, 21):
                        pe.wait_ge(x_ready, g * 160 + (l + 1) * 32 + n - 4)
                        channels(n)
                    finish(1)

                def fc2(n):
                    o, hb, s = n // 32, n // 2 % 16, n % 2
                    c0 = 63 - (32 * s + hb)
                    pe.wait_ge(gh_sb, g * 64 + n + 1)
                    mm(bank(ACC[o]), r(fc2_w[:, c0:c0 + 128]), r(slot(gh, n)), start=n % 32 == 0, stop=False)
                    pe.wait_ge(gl_sb, g * 64 + n + 1)
                    mm(bank(ACC[o]), r(fc2_w[:, c0:c0 + 128]), r(slot(gl, n)), start=False,
                       stop=n % 32 == 31).then_inc(fc2_ps, 1)

                def add_parts(o):
                    pe.wait_ge(acc_sb, g * 2 + o + 1)
                    mm(bank(3)[64 * o:64 * o + 64, :], fold, acc, start=True, stop=True).then_inc(fold_ps, 1)

                pe.wait_ge(fc_split, g + 1)
                for n in range(4 * G):
                    nb, part = n // 2, slice(128 * (n % 2), 128 * (n % 2) + 128)
                    if n < 4:
                        pe.wait_ge(x_ready, g * 160 + (156, 157, 159, 160)[n])
                    else:
                        pe.wait_ge(g_sb, g * 64 + n - 3)
                    if n % 2 == 0:
                        pe.wait_ge(xh_sb, g * 32 + nb + 1)
                    o = bank(FC1_RING[n % 4])
                    mm(o, r(fc_hi[:, part]), r(slot(xh, nb)), start=True, stop=False)
                    mm(o, r(fc1_lo[:, part]), r(slot(xh, nb)), start=False, stop=False)
                    if n % 2 == 0:
                        pe.wait_ge(xl_sb, g * 32 + nb + 1)
                    mm(o, r(fc_hi[:, part]), r(slot(xl, nb)), start=False, stop=True).then_inc(fc1_ps, 1)
                    if n >= 3:
                        fc2(n - 3)
                    if n == 39:
                        add_parts(0)
                for n in range(4 * G - 3, 4 * G):
                    fc2(n)
                add_parts(1)
                pe.wait_ge(ht_sb, g + 1)

        @block.scalar
        def _(act):
            act.wait_ge(consts, 16 * NCONST)
            with act.Fori(0, GROUPS) as g:
                for n in range(2 * G):
                    act.wait_ge(fc0_ps, g * 32 + n + 1)
                    nc.scalar.activation(xcols(n), bank8(4 + n % 4), ACT.Identity,
                                         bias=fc0_b).then_inc(x_ready, 1)
                with act.Fori(0, LAYERS) as l:
                    it = g * LAYERS + l
                    act.wait_ge(w_spread, it * 15 + 5)
                    for n in range(32):
                        u, k = divmod(n, 8)
                        act.wait_ge(y_ps, it * 32 + n + 1)
                        dst = Y[:, k * 1280:(k + 1) * 1280].rearrange("p (c k i) -> p c i k", c=2, k=KR)
                        src = bank(Y_RING[n % 4])[:, 0:320].rearrange("p (c i k) -> p c i k", c=2, i=J)
                        nc.scalar.activation(dst[:, :, u:u + 13:4], src, ACT.Identity).then_inc(y_sb, 1)
                    for n in range(15):
                        tt, a = divmod(n, 5)
                        w = 256 if tt < 2 else 128
                        c0 = a * 640 + 256 * tt
                        act.wait_ge(s_sb, it * 15 + n + 1)
                        nc.scalar.mul(Sn[:, c0:c0 + w], S[:, c0:c0 + w], -1.0).then_inc(sn_sb, 1)
                    act.wait_ge(layer_w, it * 16 + 16)
                    for n in range(32):
                        act.wait_ge(o_ps, it * 32 + n + 1)
                        nc.scalar.activation(x[:, 512 * n:512 * n + 512], bank(OUT_RING[n % 5]), ACT.Gelu,
                                             bias=cb).then_inc(x_ready, 1)
                for n in range(4 * G):
                    act.wait_ge(fc1_ps, g * 64 + n + 1)
                    if n >= 4:
                        act.wait_ge(gl_sb, g * 64 + n - 3)
                    nc.scalar.activation(slot(gel, n), bank(FC1_RING[n % 4]), ACT.Gelu,
                                         bias=fc1_b).then_inc(g_sb, 1)

        @block.vector
        def _(dve):
            nc.vector.memset(xin[:, 0:2048], 0.0).then_inc(zeroed, 1)
            nc.vector.memset(Xt[64:128, 2 * 1280:3 * 1280], 0.0)
            dve.wait_ge(consts, 16 * NCONST)

            def turn(u, ready=None, quarter=None):
                if ready is not None:
                    dve.wait_ge(x_ready, ready)
                for q in range(4) if quarter is None else [quarter]:
                    wh, hh = divmod(q, 2)
                    src = x[:, u // 2 * OCT:(u // 2 + 1) * OCT].rearrange(
                        "p (h i v w) -> p i v h w", h=HW, i=2, v=2)[:, u % 2, wh, 32 * hh:32 * hh + 32, :]
                    dst = T[u % 2][:, 2048 * wh:2048 * wh + 2048].rearrange(
                        "p (c h) -> p h c", c=CH)[:, 32 * hh:32 * hh + 32, :]
                    nc.vector.transpose(dst, src).then_inc(t_sb, 1)

            with dve.Fori(0, GROUPS) as g:
                turn(0, g * 160 + 16)
                with dve.Fori(0, LAYERS) as l:
                    it = g * LAYERS + l
                    turn(1, g * 160 + l * 32 + 32)
                    for u in range(2, 4):
                        dve.wait_ge(y_ps, it * 32 + 8 * (u - 1))
                        turn(u)
                    for n in range(12):
                        tt, k = divmod(n, 4)
                        M = 128 if tt < 2 else 64
                        if n == 8:
                            dve.wait_ge(xt_sb, it * 3 + 1)
                        dve.wait_ge(f2_ps, it * 12 + n + 1)
                        c0 = tt % 2 * 1280
                        dst = F2[0:M, c0:c0 + 1280].rearrange("p (k g c) -> p g c k", g=CH // 2, c=2)
                        src = bank(F2_RING[n % 4])[0:M, 0:4 * NW].rearrange("p (g m) -> p g m", g=4)[:, :, 0:80].rearrange(
                            "p g (c k) -> p g c k", c=2)
                        nc.vector.tensor_copy(dst[:, 4 * k:4 * k + 4], src).then_inc(f2_sb, 1)
                        if k == 3:
                            dve.wait_ge(f2_sb, it * 12 + n + 1)
                            dst = Xt[0:M, tt * 1280:(tt + 1) * 1280].rearrange("p (x k r i) -> p r x k i",
                                                                               x=MODES, k=4, r=2)
                            for ri in range(2):
                                m = nc.vector.transpose(dst[:, ri], F2[0:M, c0 + 640 * ri:c0 + 640 * ri + 640])
                            m.then_inc(xt_sb, 1)
                    dve.wait_ge(xt_sb, it * 3 + 3)
                    dve.wait_ge(layer_w, it * 16 + 16)
                    nc.vector.tensor_copy(r(cw_hi), cw).then_inc(cwh_sb, 1)

                    def split_x(n):
                        if n >= 3:
                            dve.wait_ge(mixed, it * 32 + n - 2)
                        src = x[:, 512 * n:512 * n + 512]
                        nc.vector.tensor_copy(r(ch[n % 3]), src).then_inc(ch_sb, 1)
                        dve.wait_ge(ch_sb, it * 32 + n + 1)
                        nc.vector.tensor_tensor(r(cl[n % 3]), src, ch[n % 3], ALU.subtract).then_inc(cl_sb, 1)

                    for n in range(15):
                        tt, a = divmod(n, 5)
                        w = 256 if tt < 2 else 128
                        dve.wait_ge(mix_ps, it * 15 + n + 1)
                        c0 = a * 640 + 256 * tt
                        nc.vector.tensor_copy(S[:, c0:c0 + w], bank(S_RING[n % 4])[:, 0:w]).then_inc(s_sb, 1)
                        if n == 0:
                            dve.wait_ge(cwh_sb, it + 1)
                            nc.vector.tensor_tensor(r(cw_lo), cw, cw_hi, ALU.subtract).then_inc(cw_sb, 1)
                        if n in (3, 6):
                            split_x(n // 3 - 1)
                    dve.wait_ge(w_spread, it * 15 + 15)
                    for n in range(2, 5):
                        split_x(n)
                    for n in range(32):
                        qd, k = divmod(n, 8)
                        if n == 16:
                            dve.wait_ge(o_ps, it * 32 + 16)
                        dve.wait_ge(z_ps, it * 32 + n + 1)
                        dst = Z[0:VR, :].rearrange("p (h r o) -> p o r h", h=HW, r=J)[:, :, qd % 2::2]
                        src = bank(Z_RING[n % 3])[0:VR, :].rearrange("p (o r h) -> p o r h", o=4, r=2)
                        nc.vector.tensor_copy(dst[:, 4 * k:4 * k + 4], src).then_inc(z_sb, 1)
                        if n == 15:
                            for m in range(5, 16):
                                split_x(m)
                        if n in (18, 21, 24):
                            split_x(n // 3 + 10)
                    for n in range(19, 2 * G):
                        split_x(n)
                        if n in (22, 24, 26, 28):
                            turn(0, g * 160 + l * 32 + 48, n // 2 - 11)
                dve.wait_ge(fc_loaded, g * 16 + 16)
                nc.vector.tensor_copy(r(fc_hi), fc_raw).then_inc(fc_cut, 1)
                dve.wait_ge(fc_cut, g + 1)
                nc.vector.tensor_tensor(r(fc1_lo), fc_raw[:, 0:256], fc_hi[:, 0:256], ALU.subtract)
                nc.vector.tensor_tensor(r(fc2_w[:, 100:191]), fc_raw[:, 356:FC], fc_hi[:, 356:FC], ALU.subtract)
                nc.vector.tensor_copy(r(fc2_w[:, 0:100]), fc_raw[:, 256:356]).then_inc(fc_split, 1)

                def high_x(nb):
                    if nb >= 4:
                        dve.wait_ge(fc1_ps, g * 64 + 2 * (nb - 3))
                    dve.wait_ge(x_ready, g * 160 + 128 + nb + 1)
                    nc.vector.tensor_copy(r(slot(xh, nb)), x[:, 512 * nb:512 * nb + 512]).then_inc(xh_sb, 1)

                high_x(0)
                high_x(1)
                for n in range(4 * G):
                    if n >= 4:
                        dve.wait_ge(fc2_ps, g * 64 + n - 3)
                    dve.wait_ge(g_sb, g * 64 + n + 1)
                    nc.vector.tensor_copy(r(slot(gh, n)), slot(gel, n)).then_inc(gh_sb, 1)
                    if n % 2 == 0 and n // 2 + 2 < 2 * G:
                        high_x(n // 2 + 2)
                    dve.wait_ge(gh_sb, g * 64 + n + 1)
                    nc.vector.tensor_tensor(r(slot(gl, n)), slot(gel, n), slot(gh, n), ALU.subtract).then_inc(gl_sb, 1)
                    if n in (35, 63):
                        o = n // 63
                        dve.wait_ge(fc2_ps, g * 64 + 32 * (o + 1))
                        if o:
                            dve.wait_ge(fold_ps, g * 2 + 1)
                        nc.vector.tensor_copy(acc, bank(ACC[o])).then_inc(acc_sb, 1)
                dve.wait_ge(fold_ps, g * 2 + 2)
                nc.vector.tensor_scalar(ht.rearrange("p (i h w) -> p h i w", i=2, h=4),
                                        bank(3).rearrange("p (h i w) -> p h i w", h=4, i=2),
                                        fc2_b, None, ALU.add).then_inc(ht_sb, 1)
                dve.wait_ge(h_stored, g * 32 + 32)


def tail(nc, t, out):
    with ExitStack() as ctx:
        def sem(name):
            return ctx.enter_context(nc.semaphore(name))

        def sb(name, n):
            return ctx.enter_context(nc.sbuf_tensor(name, [128, n], F32))[:, :]

        ps = ctx.enter_context(nc.psum_tensor("tail_ps", [128, 8, 512], F32))
        H, K, Vv, R = sb("H", N), sb("K", N), sb("Vv", N), sb("R", N)
        hid = sb("hid", 4 * N)
        A1, A2, A3, A4 = (hid[:, i * N:(i + 1) * N] for i in range(4))
        hT = sb("hT", N)
        ident, wkvr, wo, wr = sb("t_id", 128), sb("wkvr", 384), sb("wo", 128), sb("wr", 128)
        wk_f, wv_f, w1, wg, wd = sb("wk_f", HID), sb("wv_f", 128), sb("w1", HID), sb("wg", 2 * E), sb("wd", 2 * E * CT)
        b1m = sb("b1m", 2)
        bd_diag, bg_bc, gT = sb("bd_diag", 16 * CT), sb("bg_bc", E), sb("gT", 512)
        g1, b1, g2, b2 = sb("g1", 1), sb("b1", 1), sb("g2", 1), sb("b2", 1)
        dec, fst = sb("dec", CT), sb("fst", CT)
        mean, var, rstd = sb("mean", T64), sb("var", T64), sb("rstd", T64)
        lg, gate = sb("lg", T64 * E), sb("gate", T64 * E)
        rank, mx, sm = sb("rank", E), sb("mx", T64), sb("sm", T64)
        kk = sb("kk", 4096)
        rl = sb("rl", 1024)
        prod = sb("prod", 1024)

        h_in, w_in, cleared, stored = sem("h_in"), sem("w_in"), sem("cleared"), sem("stored")
        v = sem("dve_step")
        tp_done, hT_done = sem("tp_done"), sem("hT_done")
        r_ps = sem("r_ps")
        kvr_ps, kvr_sb, sig_sb = sem("kvr_ps"), sem("kvr_sb"), sem("sig_sb")
        wo_ps, wo_sb, r2_ps, r2_sb = sem("wo_ps"), sem("wo_sb"), sem("r2_ps"), sem("r2_sb")
        kf_ps, rl_sb, kk_sb, vf_ps, vf_sb = sem("kf_ps"), sem("rl_sb"), sem("kk_sb"), sem("vf_ps"), sem("vf_sb")
        w1_ps, hid_sb, lg_ps, lg_sb = sem("w1_ps"), sem("hid_sb"), sem("lg_ps"), sem("lg_sb")
        ex_ps, prod_sb, moe_sb = sem("ex_ps"), sem("prod_sb"), sem("moe_sb")
        neg_half, half_in = sb("neg_half", T64), sem("half_in")
        var_in, rstd_in = sem("var_in"), sem("rstd_in")
        ln_in, scan_in = sem("ln_in"), sem("scan_in")
        gate_in, gT_ps, gT_sb, bd_ps, bd_sb = sem("gate_in"), sem("gT_ps"), sem("gT_sb"), sem("bd_ps"), sem("bd_sb")
        logits_in, out_ready, exp_sb = sem("logits_in"), sem("out_ready"), sem("exp_sb")
        NWIN = 1 + 2 * (3 + 4 + 4) + 2 * 4 + 16 + 3
        block = ctx.enter_context(nc.Block())

        def bank(i):
            return ps[:, i, :]

        def tc(ap):
            return ap.rearrange("p (t c) -> p t c", t=T64)

        def ct(ap):
            return ap.rearrange("p (c t) -> p c t", c=CT)

        def over_c(ap):
            return ap.rearrange("p (t o) -> p t o", o=1).to_broadcast([128, T64, CT])

        @block.sync
        def _(sp):
            sp.dma_start(H, t["hs"].rearrange("g r i s f -> (g r i) (s f)")).then_inc(h_in, 16)
            sp.wait_ge(cleared, 1)
            sp.dma_start(ident, t["t_ident"]).then_inc(w_in, 16)
            for t2 in range(2):
                q = slice(64 * t2, 64 * t2 + 64)
                for i, w in enumerate(("Wk", "Wv", "Wr")):
                    c0 = 128 * i + 64 * t2
                    sp.dma_start(wkvr[q, c0:c0 + 64], t["L0_attn_" + w]).then_inc(w_in, 16)
                sp.dma_start(wo[q, q], t["L0_attn_Wo"]).then_inc(w_in, 16)
                sp.dma_start(wr[q, q], t["L0_attn_Wr_ffn"]).then_inc(w_in, 16)
                sp.dma_start(wk_f[q, :], t["L0_attn_Wk_ffn"]).then_inc(w_in, 16)
                sp.dma_start(w1[q, :], t["L0_ffn_W1"]).then_inc(w_in, 16)
                for dst, w in ((g1, "attn_g1"), (b1, "attn_b1"), (g2, "attn_g2"), (b2, "attn_b2")):
                    sp.dma_start(dst[q, :], t["L0_" + w].rearrange("(c o) -> c o", o=1)).then_inc(w_in, 16)
            for m in range(2):
                h = slice(128 * m, 128 * m + 128)
                sp.dma_start(wv_f[:, 64 * m:64 * m + 64], t["L0_attn_Wv_ffn"][h, :]).then_inc(w_in, 16)
                sp.dma_start(wg[:, E * m:E * m + E], t["L0_ffn_Wg"][h, :]).then_inc(w_in, 16)
                sp.dma_start(b1m[:, m:m + 1], t["L0_ffn_b1"][h].rearrange("(c o) -> c o", o=1)).then_inc(w_in, 16)
                sp.dma_start(wd[:, 512 * m:512 * m + 512].rearrange("p (e c) -> p e c", e=E),
                             t["L0_ffn_Wd"][:, h, :].rearrange("e p c -> p e c")).then_inc(w_in, 16)
            for i in range(16):
                sp.dma_start(bd_diag[E * i:E * i + E, CT * i:CT * i + CT], t["L0_ffn_bd"]).then_inc(w_in, 16)
            for dst, w in ((bg_bc, t["L0_ffn_bg"]),
                           (dec, t["L0_attn_spatial_decay"]), (fst, t["L0_attn_spatial_first"])):
                sp.dma_start(dst, w.rearrange("(o n) -> o n", o=1).to_broadcast([128, dst.shape[1]])).then_inc(w_in, 16)
            sp.wait_ge(out_ready, 1)
            sp.dma_start(out.rearrange("b t c -> b (t c)"), A2).then_inc(stored, 16)
            sp.wait_ge(stored, 16)

        @block.vector
        def _(dve):
            n, norms = [0], [0]

            def step(ins):
                n[0] += 1
                ins.then_inc(v, 1)
                dve.wait_ge(v, n[0])

            def layer_norm(src, dst, tmp):
                step(nc.vector.tensor_reduce(mean, tc(src), AX.X, ALU.add))
                step(nc.vector.tensor_scalar(mean, mean, 1.0 / CT, None, ALU.mult))
                step(nc.vector.tensor_tensor(tc(dst), tc(src), over_c(mean), ALU.subtract))
                step(nc.vector.tensor_tensor(tmp, dst, dst, ALU.mult))
                step(nc.vector.tensor_reduce(var, tc(tmp), AX.X, ALU.add))
                step(nc.vector.tensor_scalar(var, var, 1.0 / CT, 1e-5, ALU.mult, ALU.add))
                norms[0] += 1
                nc.vector.engine_nop().then_inc(var_in, 1)
                dve.wait_ge(rstd_in, norms[0])
                step(nc.vector.tensor_tensor(tc(dst), tc(dst), over_c(rstd), ALU.mult))

            def turned(i, gain=None, bias=None):
                for k in range(8):
                    dve.wait_ge(tp_done, 8 * i + k + 1)
                    o = hT[:, 512 * k:512 * k + 512]
                    if gain is None:
                        nc.vector.tensor_copy(o, bank(k)).then_inc(hT_done, 1)
                    else:
                        nc.vector.tensor_scalar(o, bank(k), gain, bias, ALU.mult, ALU.add).then_inc(hT_done, 1)

            nc.vector.memset(wkvr, 0.0)
            nc.vector.memset(bd_diag, 0.0)
            nc.vector.memset(wo, 0.0)
            nc.vector.memset(wr, 0.0).then_inc(cleared, 1)
            for e in range(E):
                m = nc.vector.memset(rank[:, e:e + 1], float(E - e))
            step(m)
            dve.wait_ge(w_in, 16 * NWIN)
            step(nc.vector.tensor_scalar(dec, dec, 1.0 / T64, None, ALU.mult))
            step(nc.vector.tensor_scalar(fst, fst, 1.0 / T64, None, ALU.mult))
            dve.wait_ge(h_in, 16)
            layer_norm(H, A1, A2)
            nc.vector.engine_nop().then_inc(ln_in, 1)
            turned(0, g1, b1)
            for tp in range(TP):
                dve.wait_ge(kvr_ps, tp + 1)
                src = bank(tp % 4)[:, 0:256].rearrange("p (k t c) -> p k c t", k=2, t=2)
                nc.vector.tensor_copy(ct(K)[:, :, 2 * tp:2 * tp + 2], src[:, 0])
                nc.vector.tensor_copy(ct(Vv)[:, :, 2 * tp:2 * tp + 2], src[:, 1]).then_inc(kvr_sb, 1)
            dve.wait_ge(kvr_sb, TP)
            late, early = slice(1, T64), slice(0, T64 - 1)
            tt = nc.vector.tensor_tensor
            per_c = lambda ap, n_: ap.rearrange("p (c o) -> p c o", o=1).to_broadcast([128, CT, n_])
            step(nc.vector.tensor_copy(ct(A1), per_c(dec, T64)))
            step(nc.vector.memset(ct(A1)[:, :, 0:1], NEG))
            step(nc.vector.tensor_tensor_scan(A2, A1, K, NEG, ALU.add, ALU.max))
            step(tt(A3, A1, A2, ALU.subtract))
            step(tt(ct(A3)[:, :, late], ct(A3)[:, :, late], ct(A2)[:, :, early], ALU.add))
            step(tt(ct(A4), ct(K), per_c(fst, T64), ALU.add))
            step(nc.vector.tensor_copy(A1, A4))
            step(tt(ct(A1)[:, :, late], ct(A4)[:, :, late], ct(A2)[:, :, early], ALU.max))
            step(tt(A4, A4, A1, ALU.subtract))
            step(tt(ct(A1)[:, :, late], ct(A2)[:, :, early], ct(A1)[:, :, late], ALU.subtract))
            step(nc.vector.memset(ct(A1)[:, :, 0:1], NEG))
            step(tt(K, K, A2, ALU.subtract))
            nc.vector.engine_nop().then_inc(scan_in, 1)
            dve.wait_ge(exp_sb, 4)
            dve.wait_ge(sig_sb, TP)
            step(tt(hT, K, Vv, ALU.mult))
            step(nc.vector.tensor_tensor_scan(A2, A3, hT, 0.0, ALU.mult, ALU.add))
            step(nc.vector.tensor_tensor_scan(hT, A3, K, 0.0, ALU.mult, ALU.add))
            step(tt(A3, A4, Vv, ALU.mult))
            step(tt(ct(A2)[:, :, early], ct(A1)[:, :, late], ct(A2)[:, :, early], ALU.mult))
            step(tt(ct(A3)[:, :, late], ct(A3)[:, :, late], ct(A2)[:, :, early], ALU.add))
            step(tt(ct(hT)[:, :, early], ct(A1)[:, :, late], ct(hT)[:, :, early], ALU.mult))
            step(tt(ct(A4)[:, :, late], ct(A4)[:, :, late], ct(hT)[:, :, early], ALU.add))
            step(nc.vector.reciprocal(A4, A4))
            step(tt(A3, A3, A4, ALU.mult))
            step(tt(tc(A1), tc(R), ct(A3).rearrange("p c t -> p t c"), ALU.mult))
            nc.vector.engine_nop().then_inc(ln_in, 1)
            turned(1)
            for k in range(8):
                dve.wait_ge(wo_ps, k + 1)
                c = slice(512 * k, 512 * k + 512)
                tt(A2[:, c], H[:, c], bank(k), ALU.add).then_inc(wo_sb, 1)
            dve.wait_ge(wo_sb, 8)
            layer_norm(A2, A1, A3)
            nc.vector.engine_nop().then_inc(ln_in, 1)
            turned(2, g2, b2)
            for f in range(32):
                i = f // 4
                dve.wait_ge(rl_sb, f + 1)
                if i >= 2 and f % 4 == 0:
                    dve.wait_ge(vf_ps, i - 1)
                r = rl[:, f % 2 * 512:f % 2 * 512 + 512]
                tt(kk[:, f % 8 * 512:f % 8 * 512 + 512], r, r, ALU.mult).then_inc(kk_sb, 1)
                if f % 4 == 3:
                    dve.wait_ge(vf_ps, i + 1)
                    c = slice(512 * i, 512 * i + 512)
                    tt(A3[:, c], R[:, c], bank(6 + i % 2), ALU.mult).then_inc(vf_sb, 1)
            dve.wait_ge(vf_sb, 8)
            step(tt(A2, A2, A3, ALU.add))
            step(tt(H, H, A2, ALU.add))
            layer_norm(H, K, Vv)
            nc.vector.engine_nop().then_inc(ln_in, 1)
            turned(3)
            for k in range(8):
                dve.wait_ge(lg_ps, k + 1)
                c = slice(64 * k, 64 * k + 64)
                tt(lg[:, c].rearrange("p (t e) -> p t e", e=E), bank(6 + k % 2)[:, 0:64].rearrange("p (t e) -> p t e", e=E),
                   bg_bc.rearrange("p (o e) -> p o e", o=1).to_broadcast([128, 8, E]), ALU.add).then_inc(lg_sb, 1)
            dve.wait_ge(lg_sb, 8)
            te = lambda ap: ap.rearrange("p (t e) -> p t e", e=E)
            over_e = lambda ap: ap.rearrange("p (t o) -> p t o", o=1).to_broadcast([128, T64, E])
            step(nc.vector.tensor_reduce(mx, te(lg), AX.X, ALU.max))
            step(tt(te(lg), te(lg), over_e(mx), ALU.subtract))
            nc.vector.engine_nop().then_inc(logits_in, 1)
            dve.wait_ge(exp_sb, 5)
            step(nc.vector.tensor_reduce(sm, te(lg), AX.X, ALU.add))
            step(nc.vector.reciprocal(sm, sm))
            step(tt(te(lg), te(lg), over_e(sm), ALU.mult))
            step(nc.vector.tensor_reduce(mx, te(lg), AX.X, ALU.max))
            step(tt(te(gate), te(lg), over_e(mx), ALU.is_equal))
            step(tt(te(gate), te(gate), rank.rearrange("p (o e) -> p o e", o=1).to_broadcast([128, T64, E]), ALU.mult))
            step(nc.vector.tensor_reduce(sm, te(gate), AX.X, ALU.max))
            step(tt(te(gate), te(gate), over_e(sm), ALU.is_equal))
            step(tt(te(gate), te(gate), over_e(mx), ALU.mult))
            nc.vector.engine_nop().then_inc(gate_in, 1)
            dve.wait_ge(gT_ps, 1)
            nc.vector.tensor_copy(gT, bank(4)).then_inc(gT_sb, 1)
            for k in range(8):
                dve.wait_ge(bd_ps, k + 1)
                c = slice(512 * k, 512 * k + 512)
                tt(K[:, c], K[:, c], bank(k), ALU.add).then_inc(bd_sb, 1)
            dve.wait_ge(bd_sb, 8)
            for i in range(T64):
                dve.wait_ge(ex_ps, i + 1)
                p = prod[:, i % 2 * 512:i % 2 * 512 + 512]
                pe_ = p.rearrange("p (e c) -> p e c", e=E)
                tt(pe_, bank(i % 4).rearrange("p (e c) -> p e c", e=E),
                   gate[:, E * i:E * i + E].rearrange("p (e o) -> p e o", o=1).to_broadcast([128, E, CT]),
                   ALU.mult).then_inc(prod_sb, 1)
                dve.wait_ge(prod_sb, i + 1)
                nc.vector.tensor_reduce(Vv[:, CT * i:CT * i + CT], p.rearrange("p (e c) -> p c e", e=E),
                                        AX.X, ALU.add).then_inc(moe_sb, 1)
            dve.wait_ge(moe_sb, T64)
            step(tt(K, K, Vv, ALU.add))
            layer_norm(K, A2, A3)
            nc.vector.engine_nop().then_inc(out_ready, 1)

        @block.tensor
        def _(pe):
            mm = nc.tensor.matmul

            def turn(i, src):
                pe.wait_ge(ln_in, i + 1)
                for k in range(8):
                    for j in range(4):
                        c0 = 512 * k + 128 * j
                        m = nc.tensor.transpose(bank(k)[:, 128 * j:128 * j + 128], src[:, c0:c0 + 128], ident)
                    m.then_inc(tp_done, 1)

            def pair(tp):
                return hT[:, 128 * tp:128 * tp + 128]

            pe.wait_ge(w_in, 16 * NWIN)
            turn(0, A1)
            pe.wait_ge(hT_done, 8)
            for tp in range(TP):
                if tp >= 4:
                    pe.wait_ge(kvr_sb, tp - 3)
                    pe.wait_ge(sig_sb, tp - 3)
                mm(bank(tp % 4)[:, 0:256], pair(tp), wkvr[:, 0:256], start=True, stop=True).then_inc(kvr_ps, 1)
                mm(bank(4 + tp % 4)[:, 0:128], pair(tp), wkvr[:, 256:384], start=True, stop=True).then_inc(r_ps, 1)
            pe.wait_ge(sig_sb, TP)
            pe.wait_ge(kvr_sb, TP)
            turn(1, A1)
            for k in range(8):
                pe.wait_ge(hT_done, 8 + k + 1)
                for j in range(4):
                    m = mm(bank(k)[:, 128 * j:128 * j + 128], pair(4 * k + j), wo, start=True, stop=True)
                m.then_inc(wo_ps, 1)
            pe.wait_ge(wo_sb, 8)
            turn(2, A1)
            pe.wait_ge(hT_done, 24)
            for k in range(8):
                for j in range(4):
                    m = mm(bank(k)[:, 128 * j:128 * j + 128], pair(4 * k + j), wr, start=True, stop=True)
                m.then_inc(r2_ps, 1)
            pe.wait_ge(r2_sb, 8)

            def hidden(i, w, filled, emptied):
                for k in range(4):
                    f = 4 * i + k
                    t2, m = divmod(k, 2)
                    q = slice(64 * t2, 64 * t2 + 64)
                    if f >= 4:
                        pe.wait_ge(emptied, f - 3)
                    mm(bank(f % 4), w[q, 128 * m:128 * m + 128], hT[q, 512 * i:512 * i + 512],
                       start=True, stop=True).then_inc(filled, 1)

            hidden(0, wk_f, kf_ps, rl_sb)
            for i in range(8):
                if i < 7:
                    hidden(i + 1, wk_f, kf_ps, rl_sb)
                pe.wait_ge(kk_sb, 4 * i + 4)
                if i >= 2:
                    pe.wait_ge(vf_sb, i - 1)
                for j in range(8):
                    for m in range(2):
                        c0 = (4 * (i % 2) + 2 * (j % 2) + m) * 512 + 128 * (j // 2)
                        ins = mm(bank(6 + i % 2)[:, CT * j:CT * j + CT], kk[:, c0:c0 + 128],
                                 wv_f[:, CT * m:CT * m + CT], start=m == 0, stop=m == 1)
                ins.then_inc(vf_ps, 1)
            turn(3, K)
            pe.wait_ge(hT_done, 32)
            hidden(0, w1, w1_ps, hid_sb)
            for i in range(8):
                if i < 7:
                    hidden(i + 1, w1, w1_ps, hid_sb)
                pe.wait_ge(hid_sb, 4 * i + 4)
                if i >= 2:
                    pe.wait_ge(lg_sb, i - 1)
                for j in range(8):
                    for m in range(2):
                        c0 = m * 2 * N + (8 * i + j) * 128
                        ins = mm(bank(6 + i % 2)[:, E * j:E * j + E], hid[:, c0:c0 + 128],
                                 wg[:, E * m:E * m + E], start=m == 0, stop=m == 1)
                ins.then_inc(lg_ps, 1)
            pe.wait_ge(gate_in, 1)
            for k in range(4):
                m = nc.tensor.transpose(bank(4)[:, 128 * k:128 * k + 128], gate[:, 128 * k:128 * k + 128], ident)
            m.then_inc(gT_ps, 1)
            pe.wait_ge(gT_sb, 1)
            for k in range(8):
                mm(bank(k), gT[:, 128 * (k // 2):128 * (k // 2) + 128], bd_diag[:, 512 * (k % 2):512 * (k % 2) + 512],
                   start=True, stop=True).then_inc(bd_ps, 1)
            pe.wait_ge(bd_sb, 8)
            for i in range(T64):
                if i >= 4:
                    pe.wait_ge(prod_sb, i - 3)
                for m in range(2):
                    c0 = m * 2 * N + i * 128
                    ins = mm(bank(i % 4), hid[:, c0:c0 + 128], wd[:, 512 * m:512 * m + 512],
                             start=m == 0, stop=m == 1)
                ins.then_inc(ex_ps, 1)

        @block.gpsimd
        def _(pool):
            nc.gpsimd.memset(neg_half, -0.5).then_inc(half_in, 1)
            pool.wait_ge(half_in, 1)
            for i in range(4):
                pool.wait_ge(var_in, i + 1)
                nc.gpsimd.tensor_tensor(rstd, var, neg_half, ALU.pow).then_inc(rstd_in, 1)

        @block.scalar
        def _(act):
            for tp in range(TP):
                act.wait_ge(r_ps, tp + 1)
                nc.scalar.activation(R[:, 128 * tp:128 * tp + 128], bank(4 + tp % 4)[:, 0:128],
                                     ACT.Sigmoid).then_inc(sig_sb, 1)
            act.wait_ge(scan_in, 1)
            for ap in (A3, A1, A4, K):
                nc.scalar.activation(ap, ap, ACT.Exp).then_inc(exp_sb, 1)
            for k in range(8):
                act.wait_ge(r2_ps, k + 1)
                nc.scalar.activation(R[:, 512 * k:512 * k + 512], bank(k), ACT.Sigmoid).then_inc(r2_sb, 1)
            for f in range(32):
                act.wait_ge(kf_ps, f + 1)
                if f >= 2:
                    act.wait_ge(kk_sb, f - 1)
                nc.scalar.activation(rl[:, f % 2 * 512:f % 2 * 512 + 512], bank(f % 4), ACT.Relu).then_inc(rl_sb, 1)
            act.wait_ge(w_in, 16 * NWIN)
            for f in range(32):
                i, t2, m = f // 4, f // 2 % 2, f % 2
                act.wait_ge(w1_ps, f + 1)
                c0 = m * 2 * N + i * 1024
                dst = hid[:, c0:c0 + 1024].rearrange("p (j t b) -> p t j b", j=4, t=2)[:, t2]
                nc.scalar.activation(dst, bank(f % 4).rearrange("p (j b) -> p j b", j=4), ACT.Gelu,
                                     bias=b1m[:, m:m + 1]).then_inc(hid_sb, 1)
            act.wait_ge(logits_in, 1)
            nc.scalar.activation(lg, lg, ACT.Exp).then_inc(exp_sb, 1)


def build(nc, t, out):
    tokenizer(nc, t)
    tail(nc, t, out)


def laid_out(inputs):
    a = {k: np.asarray(v) for k, v in inputs.items()}
    d = {"x": a["x"].reshape(GROUPS_ALL, OCTS, J, 2, 4, 1024, 3).transpose(0, 1, 3, 4, 2, 6, 5).reshape(
        GROUPS_ALL, OCTS, 2, 4, 3 * J, 1024)}
    d["sw"] = np.stack([a[f"L0_tok_sw{l % LAYERS}"].reshape(CH, CH, 4, 5, 10, 2).transpose(4, 0, 3, 2, 5, 1).reshape(
        10 * CH, 5 * 8 * CH) for l in range(LAYERS + 1)])
    F = a["x"].dtype
    d["fc0_w"] = np.zeros((128, 128), F)
    for j in range(J):
        d["fc0_w"][3 * j:3 * j + 3, CH * j:CH * j + CH] = a["L0_tok_fc0_w"]
    d["cwb"] = np.zeros((LAYERS, 128, 129), F)
    for l in range(LAYERS):
        for j in range(J):
            q = slice(CH * j, CH * j + CH)
            d["cwb"][l, q, q], d["cwb"][l, q, 128] = a[f"L0_tok_cw{l}"].T, a[f"L0_tok_cb{l}"]
    w1, w2 = a["L0_tok_fc1_w"], a["L0_tok_fc2_w"].reshape(64)
    d["fc_w"] = np.zeros((128, FC), F)
    for j in range(J):
        s, jj = divmod(j, 2)
        d["fc_w"][CH * j:CH * j + CH, 128 * s + 64 * jj:128 * s + 64 * jj + 64] = w1
    for jj in range(2):
        for c in (63, 127):
            d["fc_w"][64 * jj:64 * jj + 64, 256 + c + 16 * jj] = w2
    d["fc_b"] = np.stack([np.tile(a["L0_tok_fc0_b"], 4), np.tile(a["L0_tok_fc1_b"], 2),
                          np.repeat(a["L0_tok_fc2_b"], 128)], axis=1)
    d.update({k: v for k, v in a.items() if k.startswith("L0_attn") or k.startswith("L0_ffn")})
    return {k: np.ascontiguousarray(v) for k, v in d.items()}


GROUPS_ALL = GROUPS


def kernel(**inputs):
    import concourse.bacc as bacc
    from concourse.bass_utils import run_bass_kernel_spmd

    nc = bacc.Bacc("TRN2", target_bir_lowering=False, num_devices=1)
    arrays = laid_out(inputs)
    arrays.update({k: np.ascontiguousarray(v.astype(np.float32)) for k, v in dft_tables().items()})
    t = {k: nc.dram_tensor(k, v.shape, F32, kind="ExternalInput").ap() for k, v in arrays.items()}
    t["hs"] = nc.dram_tensor("hs", (GROUPS, PAIRS, 2, 16, 256), F32, kind="Internal").ap()
    out = nc.dram_tensor("out", (B, HW, HW), F32, kind="ExternalOutput").ap()
    build(nc, t, out)
    r = run_bass_kernel_spmd(nc, [arrays], core_ids=[0])
    return r.results[0]["out"]
```

```python
from contextlib import ExitStack

import numpy as np

import concourse.bass as bass
from concourse import mybir

F32 = mybir.dt.float32
ALU = mybir.AluOpType
ACT = mybir.ActivationFunctionType
AX = mybir.AxisListType

B, HW, CH, MODES, LAYERS = 128, 64, 32, 20, 4
G = 16
GROUPS = B // G
PAIRS, QUADS = G // 2, G // 4
J = 4
OCTS = PAIRS // J
OCT = 2 * HW * HW
KR = 2 * MODES
HID, E = 256, 8
TP = HW // 2
T64, CT = HW, HW
N = HW * HW
NW = 96
NEG = -1e38
WARM = 64
FC = 256 + 191


def dft_tables():
    k, n = np.arange(MODES), np.arange(HW)
    ang = 2 * np.pi * np.outer(n, k) / HW
    cos, sin = np.cos(ang) / 8, np.sin(ang) / 8
    over_w = np.zeros((J, HW // 2, 2, J, 2, MODES))
    over_h = np.zeros((2, HW, 80 + NW))
    h6 = over_h[..., :160].reshape(2, HW, 2, 2, 2, MODES)
    back_h = np.zeros((128, 2, HW))
    rows = back_h[:2 * KR].reshape(2, 4, 2, 5, 2, HW)
    back_w = np.zeros((128, 2, HW))
    twice = np.where(k == 0, 1.0, 2.0)[:, None]
    for i in range(2):
        h6[i, :, 0, i, 0], h6[i, :, 0, i, 1] = cos, -sin
        h6[i, :, 1, i, 0], h6[i, :, 1, i, 1] = sin, cos
        rows[0, :, i, :, i], rows[1, :, i, :, i] = cos.T.reshape(4, 5, HW), -sin.T.reshape(4, 5, HW)
        back_w[64 * i:64 * i + KR, i] = np.concatenate([twice * cos.T, -twice * sin.T])
    for i in range(J):
        for h in range(2):
            over_w[i, :, h, i, 0], over_w[i, :, h, i, 1] = cos[32 * h:32 * h + 32], -sin[32 * h:32 * h + 32]
    return {"t_over_w": over_w.reshape(128, 2 * J * KR), "t_over_h": over_h.reshape(128, 80 + NW), "t_back_h": back_h.reshape(128, 128),
            "t_back_w": back_w.reshape(128, 128), "t_ident": np.eye(128),
            "t_fold": np.tile(np.eye(64), (2, 1)),
            "t_quads": np.repeat(np.eye(4), CH, axis=0)}


def tokenizer(nc, t):
    with ExitStack() as ctx:
        def sem(name):
            return ctx.enter_context(nc.semaphore(name))

        MODE_WORDS = CH // 2 * KR * G + 2 * 5 * MODES * CH
        fc0_w = ctx.enter_context(nc.sbuf_tensor("fc0_parts", [128, 256], F32))[:, :]
        WORDS = 53208 - 256 - MODE_WORDS
        arena = ctx.enter_context(nc.sbuf_tensor("arena", [128, WORDS], F32))
        with nc.sbuf_tensor("modes", [128, MODE_WORDS], F32) as modes:
            pass
        parts = ctx.enter_context(nc.sbuf_tensor("parts", [128, MODE_WORDS], F32))
        ps = ctx.enter_context(nc.psum_tensor("ps", [128, 8, 512], F32))
        top = [0]

        def take(n):
            top[0] += n
            assert top[0] <= WORDS, top
            return arena[:, top[0] - n:top[0]]

        over_w, over_h, back_h, back_w = take(2 * J * KR), take(80 + NW), take(128), take(128)
        cwb = take(129)
        cw, cb = cwb[:, 0:128], cwb[:, 128:129]
        biases, fold = take(3), take(64)
        fc0_b, fc1_b, fc2_b = (biases[:, i:i + 1] for i in range(3))
        x = take(OCTS * OCT)
        TW = 4096
        T = [take(TW), take(TW)]
        F2 = T[0]
        gel = T[0][:, 0:2048]
        Xt = take(3 * 1280 + 256)
        Z = arena[:, top[0] - 8192:top[0]]
        xin = [Z[:, 4096 * o:4096 * o + 4096] for o in range(OCTS)]
        VR = 64 + KR
        VROWS = VR * CH
        Y = modes[:, 0:CH // 2 * KR * G]
        V = [Y[:, i * VROWS:(i + 1) * VROWS] for i in range(2)]
        SW = 5 * 8 * CH
        stage = take(SW)
        stage_last = Y[:, 2 * VROWS:2 * VROWS + SW]
        SF = 5 * MODES * CH
        S = modes[:, MODE_WORDS - 2 * SF:MODE_WORDS - SF]
        Sn = modes[:, MODE_WORDS - SF:MODE_WORDS]
        W = [take(8 * 128) for a in range(5)] + [Y[:, a * 1024:(a + 1) * 1024] for a in range(5)]
        fc0_raw, fc_raw = S[:, 0:256], S[:, 0:FC]
        ht = S[:, 512:1024]
        fc_hi, fc1_lo, fc2_w = (parts[:, MODE_WORDS - SF + i:MODE_WORDS - SF + j]
                                for i, j in ((0, FC), (FC, FC + 256), (FC + 256, FC + 447)))
        xh, xl, gh, gl = (parts[:, 2048 * i:2048 * i + 2048] for i in range(4))
        acc = Y[:, 8192:8704]
        x0_parts = [parts[:, i:i + 512] for i in (8704, 9216, 9728)]
        SIDE = 2 * VROWS + SW
        ch, cl = ([parts[:, i + 512 * k:i + 512 * k + 512] for i in (SIDE, SIDE + 1024, 2 * VROWS)] for k in range(2))
        cw_hi, cw_lo = parts[:, SIDE + 2048:SIDE + 2176], parts[:, SIDE + 2176:SIDE + 2304]
        quads = take(4)
        gate_in, gate_out = take(1), take(1)

        NCONST = 5
        consts = sem("consts")
        gated = sem("gated")
        x_ready, tp_ps, t_sb, y_ps, y_sb = sem("x_ready"), sem("tp_ps"), sem("t_sb"), sem("y_ps"), sem("y_sb")
        f2_ps, f2_sb, xt_sb = sem("f2_ps"), sem("f2_sb"), sem("xt_sb")
        staged, w_spread, a_spread = [sem(f"staged{i}") for i in range(3)], sem("w_spread"), sem("a_spread")
        mix_ps, s_sb, sn_sb = sem("mix_ps"), sem("s_sb"), sem("sn_sb")
        v_loaded = [sem(f"v_loaded{i}") for i in range(4)]
        z_ps, z_sb, o_ps, layer_w = sem("z_ps"), sem("z_sb"), sem("o_ps"), sem("layer_w")
        xin_loaded = [sem(f"xin_loaded{i}") for i in range(4 * OCTS)]
        fc0_loaded, fc0_cut, fc0_split, fc0_ps, fc1_ps, g_sb, fc2_ps = sem("fc0_loaded"), sem("fc0_cut"), sem("fc0_split"), sem("fc0_ps"), sem("fc1_ps"), sem("g_sb"), sem("fc2_ps")
        fc_loaded, fc_cut, fc_split, acc_sb, fold_ps = (sem(n) for n in ("fc_loaded", "fc_cut", "fc_split", "acc_sb",
                                                                       "fold_ps"))
        xch_sb, xcl_sb, x_dve = sem("xch_sb"), sem("xcl_sb"), sem("x_dve")
        cwh_sb, cw_sb, ch_sb, cl_sb, mixed = sem("cwh_sb"), sem("cw_sb"), sem("ch_sb"), sem("cl_sb"), sem("mixed")
        xh_sb, xl_sb, gh_sb, gl_sb = sem("xh_sb"), sem("xl_sb"), sem("gh_sb"), sem("gl_sb")
        ht_sb, h_stored = sem("ht_sb"), sem("h_stored")

        block = ctx.enter_context(nc.Block())

        def bank(i):
            return ps[:, i, :]

        Y_RING, F2_RING, S_RING, Z_RING = (2, 3, 6, 7), (4, 5, 1, 7), (0, 2, 3, 6), (2, 3, 1)
        OUT_RING = (4, 5, 6, 7, 0)

        FC1_RING, ACC = (6, 7, 4, 5), (2, 0)

        def slot(ring, n):
            return ring[:, n % 4 * 512:n % 4 * 512 + 512]

        def r(ap):
            return ap.bitcast(mybir.dt.float32r)

        def bank8(i):
            return ps[:, i, :].rearrange("p (h w) -> p h w", h=8)

        def load_x(eng, g, pieces):
            for i in pieces:
                o, k = divmod(i, 4)
                src = t["x"][g, o, :, 1024 * k:1024 * k + 1024].rearrange("(o p) f -> o p f", o=1)
                eng.dma_start(xin[o][:, 1024 * k:1024 * k + 1024],
                              src.to_broadcast([4, 32, 1024])).then_inc(xin_loaded[i], 16)

        def xcols(c, i):
            o, k = divmod(c, 8)
            return x[:, o * OCT:(o + 1) * OCT].rearrange("p (h i w) -> p i h w", h=HW, i=2)[:, i, 8 * k:8 * k + 8, :]

        SP_V = 5

        ACT_SPREADS = {7: 4, 12: 6}
        POOL_SPREADS = {n: i + 1 for i, n in enumerate(n for n in range(15) if n not in ACT_SPREADS)}

        def spread(n, first=None, by_act=False):
            tt, a = divmod(n, 5)
            Q = 4 if tt < 2 else 2
            dst = W[n % 10].rearrange("p (m q f) -> p m q f", m=8, q=4)[:, :, 0:Q]
            src = (stage, stage, stage_last)[tt if first is None else 2][:, a * 256:(a + 1) * 256].rearrange("p (m o f) -> p m o f", m=8, o=1)
            if by_act:
                for q in range(Q):
                    nc.scalar.activation(dst[:, :, q], src[:, :, 0], ACT.Identity,
                                         scale=quads[:, q:q + 1]).then_inc(a_spread, 1)
                return
            own = quads[:, 0:Q].rearrange("p (o q u) -> p o q u", o=1, u=1)
            nc.gpsimd.tensor_tensor(dst, src.to_broadcast([128, 8, Q, CH]), own.to_broadcast([128, 8, Q, CH]),
                                    ALU.mult).then_inc(w_spread, 1)

        def load_v(eng, it, first, gate):
            eng.wait_ge(s_sb, it * 15 + 15)
            eng.wait_ge(sn_sb, it * 15 + 15)
            gate(it, 0)
            for qd in range(QUADS):
                if qd >= 2:
                    eng.wait_ge(z_ps, it * 32 + 8 * (qd - 1))
                    gate(it, qd - 1)
                for n in range(SP_V) if first else range(SP_V, 8):
                    i, kr, rr = n // 4, n // 2 % 2, n % 2
                    p0 = 8 * (kr ^ rr) + 4 * (qd % 2) + 2 * (qd // 2) + i
                    src = (Sn if kr and rr else S)[p0:p0 + 113:16, :].rearrange("p (a f) -> p a f", a=5)
                    c0 = (i * 64 + rr * MODES) * CH
                    eng.dma_start(V[qd % 2][KR * kr:KR * kr + KR, c0:c0 + MODES * CH],
                                  src).then_inc(v_loaded[2 * (1 - first) + qd % 2], 16)

        @block.gpsimd
        def _(pool):
            def gate(it, i):
                pool.wait_ge(gated, it * 3 + i + 1)
                nc.gpsimd.tensor_tensor(gate_out, gate_in, gate_in, ALU.add).then_inc(gated, 1)

            nc.gpsimd.memset(gate_in, 0.0).then_inc(gated, 1)
            pool.wait_ge(gated, 1)
            pool.wait_ge(fc0_loaded, 48)
            pool.wait_ge(staged[0], 16)
            for n in range(5):
                spread(n, True)
            with pool.Fori(0, GROUPS) as g:
                for c in range(8 * OCTS):
                    if c % 2 == 0:
                        pool.wait_ge(xin_loaded[c // 2], g * 16 + 16)
                    if c >= 3:
                        pool.wait_ge(fc0_ps, g * 32 + 2 * (c - 2))
                    nc.gpsimd.tensor_tensor(r(x0_parts[c % 3]), xin[c // 8][:, 512 * (c % 8):512 * (c % 8) + 512],
                                            gate_in.to_broadcast([128, 512]), ALU.add).then_inc(xch_sb, 1)
                with pool.Fori(0, LAYERS) as l:
                    it = g * LAYERS + l
                    pool.wait_ge(staged[1], it * 16 + 16)
                    for n in (5, 6, 8, 9):
                        pool.wait_ge(f2_ps, it * 12 + (9 if n < 7 else 10))
                        spread(n)
                    pool.wait_ge(staged[2], it * 16 + 16)
                    for n in (10, 11, 13, 14):
                        pool.wait_ge(mix_ps, it * 15 + n - 9)
                        spread(n)
                    load_v(pool, it, False, gate)
                    pool.wait_ge(staged[0], it * 16 + 32)
                    for n in range(5):
                        spread(n)
                for nb in range(2 * G):
                    if nb >= 4:
                        pool.wait_ge(fc1_ps, g * 64 + 2 * (nb - 3))
                    pool.wait_ge(xh_sb, g * 32 + nb + 1)
                    nc.gpsimd.tensor_tensor(r(slot(xl, nb)), x[:, 512 * nb:512 * nb + 512], slot(xh, nb),
                                            ALU.subtract).then_inc(xl_sb, 1)

        @block.sync
        def _(sp):
            sp.dma_start(fc0_raw, t["fc0_w"]).then_inc(fc0_loaded, 16)
            sp.dma_start(biases, t["fc_b"]).then_inc(fc0_loaded, 16)
            sp.dma_start(quads, t["t_quads"]).then_inc(fc0_loaded, 16)
            sp.dma_start(stage_last, t["sw"][0, 0:128]).then_inc(staged[0], 16)
            load_x(sp, 0, range(8))
            for dst, name in ((over_w, "t_over_w"), (over_h, "t_over_h"),
                              (back_h, "t_back_h"), (back_w, "t_back_w"), (fold, "t_fold")):
                sp.dma_start(dst, t[name]).then_inc(consts, 16)
            sp.dma_start(stage, t["sw"][0, 128:256]).then_inc(staged[1], 16)
            with sp.Fori(0, GROUPS) as g:
                with sp.Fori(0, LAYERS) as l:
                    it = g * LAYERS + l
                    sp.wait_ge(x_ready, g * 152 + l * 32 + 24)
                    sp.dma_start(cwb, t["cwb"][l]).then_inc(layer_w, 16)
                    sp.wait_ge(f2_ps, it * 12 + 12)
                    sp.dma_start(stage_last[0:64, :], t["sw"][l, 256:320]).then_inc(staged[2], 16)
                    load_v(sp, it, True, lambda it, i: None)
                    sp.wait_ge(w_spread, it * 13 + 13)
                    sp.wait_ge(a_spread, it * 6 + 4)
                    sp.dma_start(stage, t["sw"][l + 1, 0:128]).then_inc(staged[0], 16)
                    sp.wait_ge(w_spread, it * 13 + 18)
                    sp.dma_start(stage, t["sw"][l + 1, 128:256]).then_inc(staged[1], 16)
                for i, count in enumerate((SP_V, 8 - SP_V)):
                    for k in range(2):
                        sp.wait_ge(v_loaded[2 * i + k], g * 32 * LAYERS * count + 32 * LAYERS * count)
                sp.dma_start(fc_raw, t["fc_w"]).then_inc(fc_loaded, 16)
                sp.wait_ge(x_ready, g * 152 + 152)
                load_x(sp, g + 1, range(7))
                sp.wait_ge(ht_sb, g + 1)
                for i in range(2):
                    sp.dma_start(t["hs"][g, :, i], ht[:, 256 * i:256 * i + 256]).then_inc(h_stored, 16)
                sp.wait_ge(h_stored, g * 32 + 32)
                load_x(sp, g + 1, [7])
            for i in range(2):
                sp.wait_ge(staged[i], 16 * (GROUPS * LAYERS + 1))
            for i in range(4 * OCTS):
                sp.wait_ge(xin_loaded[i], 16 * (GROUPS + 1))

        @block.tensor
        def _(pe):
            mm = nc.tensor.matmul
            with pe.Fori(0, GROUPS) as g:
                pe.wait_ge(fc0_split, 2)
                for c in range(8 * OCTS):
                    if c >= 4:
                        pe.wait_ge(x_ready, g * 152 + 3 * ((c - 4) // 2) + 3)
                    pe.wait_ge(xcl_sb, g * 16 + c + 1)
                    for i in range(2):
                        mm(bank((2 * c + i + 2) % 8), r(fc0_w[:, 128 * i:128 * i + 128]), r(x0_parts[c % 3]),
                           start=True, stop=True).then_inc(fc0_ps, 1)

                with pe.Fori(0, LAYERS) as l:
                    it = g * LAYERS + l

                    pe.wait_ge(consts, 16 * NCONST)
                    for u in range(4):
                        pe.wait_ge(t_sb, g * (16 * LAYERS + 4) + l * 16 + 4 * (u + 1))
                        for k in range(8):
                            n = 8 * u + k
                            if n in (0, 2):
                                pe.wait_ge(x_ready, g * 152 + l * 32 + (24 if n else 21))
                            if n >= 4:
                                pe.wait_ge(y_sb, it * 32 + n - 3)
                            for c in range(2):
                                for wh in range(2):
                                    c0 = wh * 2048 + (2 * k + c) * 128
                                    m = mm(bank(Y_RING[n % 4])[:, 160 * c:160 * c + 160], T[u % 2][:, c0:c0 + 128],
                                           over_w[:, 160 * wh:160 * wh + 160], start=wh == 0, stop=wh == 1)
                            m.then_inc(y_ps, 1)

                    for n in range(12):
                        tt, k = divmod(n, 4)
                        M, w = (128, NW) if tt < 2 else (64, 80)
                        if tt == 0:
                            pe.wait_ge(y_sb, it * 32 + 24 + 2 * (k + 1))
                        if n >= 4:
                            pe.wait_ge(f2_sb, it * 12 + n - 3)
                        for c in range(4):
                            for ri in range(2):
                                c0 = ((4 * k + c) * 2 + ri) * MODES * G + tt * 128
                                m = mm(bank(F2_RING[n % 4])[0:M, NW * c:NW * c + w], Y[:, c0:c0 + M],
                                       over_h[:, 80 * ri:80 * ri + w], start=ri == 0, stop=ri == 1)
                        m.then_inc(f2_ps, 1)

                    for n in range(15):
                        tt, a = divmod(n, 5)
                        P = 128 if tt < 2 else 64
                        pe.wait_ge(xt_sb, it * 3 + tt + 1)
                        if n in ACT_SPREADS:
                            pe.wait_ge(a_spread, it * 6 + ACT_SPREADS[n])
                        else:
                            pe.wait_ge(w_spread, it * 13 + POOL_SPREADS[n])
                        if n >= 4:
                            pe.wait_ge(s_sb, it * 15 + n - 3)
                        for b in range(4):
                            for k2 in range(2):
                                c0 = tt * 1280 + (5 * b + a) * 64
                                lhsT = Xt[:, c0 + 32 * k2:c0 + 32 * k2 + 32]
                                o = bank(S_RING[n % 4])[32 * b:32 * b + 32, 0:2 * P].rearrange("p (q k o) -> p q k o", k=2, o=CH)
                                c1 = (2 * b + k2) * 128
                                m = mm(o[:, :, k2], lhsT, W[n % 10][:, c1:c1 + P], start=True, stop=True)
                        m.then_inc(mix_ps, 1)

                    def back_over_h(qd):
                        for i, count in enumerate((SP_V, 8 - SP_V)):
                            pe.wait_ge(v_loaded[2 * i + qd % 2], it * 32 * count + 16 * count * (qd // 2 + 1))
                        for k in range(8):
                            n = 8 * qd + k
                            if n >= 3:
                                pe.wait_ge(z_sb, it * 32 + n - 2)
                            for c in range(4):
                                m = mm(bank(Z_RING[n % 3])[0:VR, 128 * c:128 * c + 128],
                                       V[qd % 2][:, 4 * k + c:VROWS:CH], back_h, start=True, stop=True)
                            m.then_inc(z_ps, 1)

                    def channels(n):
                        o = bank(OUT_RING[n % 5])
                        pe.wait_ge(ch_sb, it * 32 + n + 1)
                        mm(o, r(cw_hi), r(ch[n % 3]), start=True, stop=False)
                        mm(o, r(cw_lo), r(ch[n % 3]), start=False, stop=False)
                        pe.wait_ge(cl_sb, it * 32 + n + 1)
                        mm(o, r(cw_hi), r(cl[n % 3]), start=False, stop=False).then_inc(mixed, 1)

                    def finish(o):
                        pe.wait_ge(z_sb, it * 32 + 16 * (o + 1))
                        for k in range(16):
                            n = 16 * o + k
                            if k >= 5:
                                pe.wait_ge(x_ready, g * 152 + l * 32 + 24 + n - 4)
                                channels(n)
                            for h in range(4):
                                z0 = (4 * k + h) * 128
                                m = mm(bank(OUT_RING[n % 5])[:, 128 * h:128 * h + 128], Z[0:VR, z0:z0 + 128],
                                       back_w[0:VR, :], start=False, stop=h == 3)
                            m.then_inc(o_ps, 1)

                    pe.wait_ge(cw_sb, it + 1)
                    for n in range(5):
                        if n == 2:
                            pe.wait_ge(s_sb, it * 15 + 15)
                        channels(n)
                    back_over_h(0)
                    back_over_h(1)
                    finish(0)
                    back_over_h(2)
                    back_over_h(3)
                    for n in range(16, 21):
                        pe.wait_ge(x_ready, g * 152 + l * 32 + 24 + n - 4)
                        channels(n)
                    finish(1)

                def fc2(n):
                    o, hb, s = n // 32, n // 2 % 16, n % 2
                    c0 = 63 - (32 * s + hb)
                    pe.wait_ge(gh_sb, g * 64 + n + 1)
                    mm(bank(ACC[o]), r(fc2_w[:, c0:c0 + 128]), r(slot(gh, n)), start=n % 32 == 0, stop=False)
                    pe.wait_ge(gl_sb, g * 64 + n + 1)
                    mm(bank(ACC[o]), r(fc2_w[:, c0:c0 + 128]), r(slot(gl, n)), start=False,
                       stop=n % 32 == 31).then_inc(fc2_ps, 1)

                def add_parts(o):
                    pe.wait_ge(acc_sb, g * 2 + o + 1)
                    mm(bank(3)[64 * o:64 * o + 64, :], fold, acc, start=True, stop=True).then_inc(fold_ps, 1)

                pe.wait_ge(fc_split, g + 1)
                for n in range(4 * G):
                    nb, part = n // 2, slice(128 * (n % 2), 128 * (n % 2) + 128)
                    if n < 4:
                        pe.wait_ge(x_ready, g * 152 + (148, 149, 151, 152)[n])
                    else:
                        pe.wait_ge(g_sb, g * 64 + n - 3)
                    if n % 2 == 0:
                        pe.wait_ge(xh_sb, g * 32 + nb + 1)
                    o = bank(FC1_RING[n % 4])
                    mm(o, r(fc_hi[:, part]), r(slot(xh, nb)), start=True, stop=False)
                    mm(o, r(fc1_lo[:, part]), r(slot(xh, nb)), start=False, stop=False)
                    if n % 2 == 0:
                        pe.wait_ge(xl_sb, g * 32 + nb + 1)
                    mm(o, r(fc_hi[:, part]), r(slot(xl, nb)), start=False, stop=True).then_inc(fc1_ps, 1)
                    if n >= 3:
                        fc2(n - 3)
                    if n == 39:
                        add_parts(0)
                for n in range(4 * G - 3, 4 * G):
                    fc2(n)
                add_parts(1)
                pe.wait_ge(ht_sb, g + 1)

        @block.scalar
        def _(act):
            act.wait_ge(fc0_loaded, 48)
            with act.Fori(0, GROUPS) as g:
                for c in range(8 * OCTS):
                    for i in range(1 + c % 2):
                        if i:
                            act.wait_ge(x_dve, g * 8 + c // 2 + 1)
                        act.wait_ge(fc0_ps, g * 32 + 2 * c + i + 1)
                        nc.scalar.activation(xcols(c, i), bank8((2 * c + i + 2) % 8), ACT.Identity,
                                             bias=fc0_b).then_inc(x_ready, 1)
                with act.Fori(0, LAYERS) as l:
                    it = g * LAYERS + l
                    act.wait_ge(consts, 16 * NCONST)
                    act.wait_ge(w_spread, it * 13 + 5)
                    for n in range(32):
                        u, k = divmod(n, 8)
                        act.wait_ge(y_ps, it * 32 + n + 1)
                        dst = Y[:, k * 1280:(k + 1) * 1280].rearrange("p (c k i) -> p c i k", c=2, k=KR)
                        src = bank(Y_RING[n % 4])[:, 0:320].rearrange("p (c i k) -> p c i k", c=2, i=J)
                        nc.scalar.activation(dst[:, :, u:u + 13:4], src, ACT.Identity).then_inc(y_sb, 1)
                    act.wait_ge(staged[1], it * 16 + 16)
                    act.wait_ge(f2_ps, it * 12 + 10)
                    spread(7, by_act=True)
                    for n in range(15):
                        tt, a = divmod(n, 5)
                        if n == 4:
                            act.wait_ge(staged[2], it * 16 + 16)
                            act.wait_ge(mix_ps, it * 15 + 3)
                            spread(12, by_act=True)
                        w = 256 if tt < 2 else 128
                        c0 = a * 640 + 256 * tt
                        act.wait_ge(s_sb, it * 15 + n + 1)
                        nc.scalar.mul(Sn[:, c0:c0 + w], S[:, c0:c0 + w], -1.0).then_inc(sn_sb, 1)
                    act.wait_ge(layer_w, it * 16 + 16)
                    for n in range(32):
                        act.wait_ge(o_ps, it * 32 + n + 1)
                        nc.scalar.activation(x[:, 512 * n:512 * n + 512], bank(OUT_RING[n % 5]), ACT.Gelu,
                                             bias=cb).then_inc(x_ready, 1)
                for n in range(4 * G):
                    act.wait_ge(fc1_ps, g * 64 + n + 1)
                    if n >= 4:
                        act.wait_ge(gl_sb, g * 64 + n - 3)
                    nc.scalar.activation(slot(gel, n), bank(FC1_RING[n % 4]), ACT.Gelu,
                                         bias=fc1_b).then_inc(g_sb, 1)

        @block.vector
        def _(dve):
            dve.wait_ge(fc0_loaded, 48)
            nc.vector.tensor_copy(r(fc0_w), fc0_raw).then_inc(fc0_cut, 1)
            dve.wait_ge(fc0_cut, 1)
            for q in (1, 3):
                p = slice(32 * q, 32 * q + 32)
                nc.vector.tensor_tensor(r(fc0_w[p]), fc0_raw[p], fc0_w[p], ALU.subtract).then_inc(fc0_split, 1)

            def turn(u, ready=None, quarter=None):
                if ready is not None:
                    dve.wait_ge(x_ready, ready)
                for q in range(4) if quarter is None else [quarter]:
                    wh, hh = divmod(q, 2)
                    src = x[:, u // 2 * OCT:(u // 2 + 1) * OCT].rearrange(
                        "p (h i v w) -> p i v h w", h=HW, i=2, v=2)[:, u % 2, wh, 32 * hh:32 * hh + 32, :]
                    dst = T[u % 2][:, 2048 * wh:2048 * wh + 2048].rearrange(
                        "p (c h) -> p h c", c=CH)[:, 32 * hh:32 * hh + 32, :]
                    nc.vector.transpose(dst, src).then_inc(t_sb, 1)

            with dve.Fori(0, GROUPS) as g:
                def x0(c):
                    dve.wait_ge(fc0_ps, g * 32 + 2 * c + 2)
                    nc.vector.tensor_scalar(xcols(c, 1), bank8((2 * c + 3) % 8), fc0_b, None, ALU.add).then_inc(x_dve, 1)

                for c in range(8 * OCTS):
                    o, k = divmod(c, 8)
                    dve.wait_ge(xch_sb, g * 16 + c + 1)
                    hi = x0_parts[c % 3][64:128, :]
                    nc.vector.tensor_tensor(r(hi), xin[o][64:128, 512 * k:512 * k + 512], hi,
                                            ALU.subtract).then_inc(xcl_sb, 1)
                    if c >= 2 and c % 2 == 0:
                        x0(c - 2)
                    if c in (11, 13, 15):
                        turn(0, g * 152 + 12, c // 2 - 5)
                x0(14)
                turn(0, quarter=3)
                with dve.Fori(0, LAYERS) as l:
                    it = g * LAYERS + l
                    turn(1, g * 152 + l * 32 + 24)
                    for u in range(2, 4):
                        dve.wait_ge(y_ps, it * 32 + 8 * (u - 1))
                        turn(u)
                    for n in range(12):
                        tt, k = divmod(n, 4)
                        M = 128 if tt < 2 else 64
                        if n == 8:
                            dve.wait_ge(xt_sb, it * 3 + 1)
                        dve.wait_ge(f2_ps, it * 12 + n + 1)
                        c0 = tt % 2 * 1280
                        dst = F2[0:M, c0:c0 + 1280].rearrange("p (k g c) -> p g c k", g=CH // 2, c=2)
                        src = bank(F2_RING[n % 4])[0:M, 0:4 * NW].rearrange("p (g m) -> p g m", g=4)[:, :, 0:80].rearrange(
                            "p g (c k) -> p g c k", c=2)
                        nc.vector.tensor_copy(dst[:, 4 * k:4 * k + 4], src).then_inc(f2_sb, 1)
                        if k == 3:
                            dve.wait_ge(f2_sb, it * 12 + n + 1)
                            dst = Xt[0:M, tt * 1280:(tt + 1) * 1280].rearrange("p (x k r i) -> p r x k i",
                                                                               x=MODES, k=4, r=2)
                            for ri in range(2):
                                m = nc.vector.transpose(dst[:, ri], F2[0:M, c0 + 640 * ri:c0 + 640 * ri + 640])
                            m.then_inc(xt_sb, 1)
                    dve.wait_ge(xt_sb, it * 3 + 3)
                    dve.wait_ge(layer_w, it * 16 + 16)
                    nc.vector.tensor_copy(r(cw_hi), cw).then_inc(cwh_sb, 1)

                    def split_x(n):
                        if n >= 3:
                            dve.wait_ge(mixed, it * 32 + n - 2)
                        src = x[:, 512 * n:512 * n + 512]
                        nc.vector.tensor_copy(r(ch[n % 3]), src).then_inc(ch_sb, 1)
                        dve.wait_ge(ch_sb, it * 32 + n + 1)
                        nc.vector.tensor_tensor(r(cl[n % 3]), src, ch[n % 3], ALU.subtract).then_inc(cl_sb, 1)

                    for n in range(15):
                        tt, a = divmod(n, 5)
                        w = 256 if tt < 2 else 128
                        dve.wait_ge(mix_ps, it * 15 + n + 1)
                        c0 = a * 640 + 256 * tt
                        nc.vector.tensor_copy(S[:, c0:c0 + w], bank(S_RING[n % 4])[:, 0:w]).then_inc(s_sb, 1)
                        if n == 0:
                            dve.wait_ge(cwh_sb, it + 1)
                            nc.vector.tensor_tensor(r(cw_lo), cw, cw_hi, ALU.subtract).then_inc(cw_sb, 1)
                        if n in (3, 6):
                            split_x(n // 3 - 1)
                    dve.wait_ge(w_spread, it * 13 + 13)
                    dve.wait_ge(a_spread, it * 6 + 6)
                    for n in range(2, 5):
                        split_x(n)
                    for n in range(32):
                        qd, k = divmod(n, 8)
                        if n == 16:
                            dve.wait_ge(o_ps, it * 32 + 16)
                        dve.wait_ge(z_ps, it * 32 + n + 1)
                        dst = Z[0:VR, :].rearrange("p (h r o) -> p o r h", h=HW, r=J)[:, :, qd % 2::2]
                        src = bank(Z_RING[n % 3])[0:VR, :].rearrange("p (o r h) -> p o r h", o=4, r=2)
                        nc.vector.tensor_copy(dst[:, 4 * k:4 * k + 4], src).then_inc(z_sb, 1)
                        if n == 15:
                            for m in range(5, 16):
                                split_x(m)
                        if n in (18, 21, 24):
                            split_x(n // 3 + 10)
                    for n in range(19, 2 * G):
                        split_x(n)
                        if n in (22, 24, 26, 28):
                            turn(0, g * 152 + l * 32 + 40, n // 2 - 11)
                dve.wait_ge(fc_loaded, g * 16 + 16)
                nc.vector.tensor_copy(r(fc_hi), fc_raw).then_inc(fc_cut, 1)
                dve.wait_ge(fc_cut, g + 1)
                nc.vector.tensor_tensor(r(fc1_lo), fc_raw[:, 0:256], fc_hi[:, 0:256], ALU.subtract)
                nc.vector.tensor_tensor(r(fc2_w[:, 100:191]), fc_raw[:, 356:FC], fc_hi[:, 356:FC], ALU.subtract)
                nc.vector.tensor_copy(r(fc2_w[:, 0:100]), fc_raw[:, 256:356]).then_inc(fc_split, 1)

                def high_x(nb):
                    if nb >= 4:
                        dve.wait_ge(fc1_ps, g * 64 + 2 * (nb - 3))
                    dve.wait_ge(x_ready, g * 152 + 120 + nb + 1)
                    nc.vector.tensor_copy(r(slot(xh, nb)), x[:, 512 * nb:512 * nb + 512]).then_inc(xh_sb, 1)

                high_x(0)
                high_x(1)
                for n in range(4 * G):
                    if n >= 4:
                        dve.wait_ge(fc2_ps, g * 64 + n - 3)
                    dve.wait_ge(g_sb, g * 64 + n + 1)
                    nc.vector.tensor_copy(r(slot(gh, n)), slot(gel, n)).then_inc(gh_sb, 1)
                    if n % 2 == 0 and n // 2 + 2 < 2 * G:
                        high_x(n // 2 + 2)
                    dve.wait_ge(gh_sb, g * 64 + n + 1)
                    nc.vector.tensor_tensor(r(slot(gl, n)), slot(gel, n), slot(gh, n), ALU.subtract).then_inc(gl_sb, 1)
                    if n in (35, 63):
                        o = n // 63
                        dve.wait_ge(fc2_ps, g * 64 + 32 * (o + 1))
                        if o:
                            dve.wait_ge(fold_ps, g * 2 + 1)
                        nc.vector.tensor_copy(acc, bank(ACC[o])).then_inc(acc_sb, 1)
                dve.wait_ge(fold_ps, g * 2 + 2)
                nc.vector.tensor_scalar(ht.rearrange("p (i h w) -> p h i w", i=2, h=4),
                                        bank(3).rearrange("p (h i w) -> p h i w", h=4, i=2),
                                        fc2_b, None, ALU.add).then_inc(ht_sb, 1)


def tail(nc, t, out):
    with ExitStack() as ctx:
        def sem(name):
            return ctx.enter_context(nc.semaphore(name))

        def sb(name, n):
            return ctx.enter_context(nc.sbuf_tensor(name, [128, n], F32))[:, :]

        ps = ctx.enter_context(nc.psum_tensor("tail_ps", [128, 8, 512], F32))
        H, K, Vv, R = sb("H", N), sb("K", N), sb("Vv", N), sb("R", N)
        hid = sb("hid", 4 * N)
        A1, A2, A3, A4 = (hid[:, i * N:(i + 1) * N] for i in range(4))
        hT = sb("hT", N)
        ident, wkvr, wo, wr = sb("t_id", 128), sb("wkvr", 384), sb("wo", 128), sb("wr", 128)
        wk_f, wv_f, w1, wg, wd = sb("wk_f", HID), sb("wv_f", 128), sb("w1", HID), sb("wg", 2 * E + WARM), sb("wd", 2 * E * CT)
        b1m = sb("b1m", 2)
        bd_diag, bg_bc, gT = sb("bd_diag", 16 * CT), sb("bg_bc", E), sb("gT", 512)
        g1, b1, g2, b2 = sb("g1", 1), sb("b1", 1), sb("g2", 1), sb("b2", 1)
        dec, fst = sb("dec", CT), sb("fst", CT)
        mean, var, std, rstd = (sb(n, T64) for n in ("mean", "var", "std", "rstd"))
        lg, gate = sb("lg", T64 * E), sb("gate", T64 * E)
        rank, mx, sm = sb("rank", E), sb("mx", T64), sb("sm", T64)
        kk = sb("kk", 4096)
        rl = sb("rl", 1024)
        prod = sb("prod", 1024)

        h_in, w_in, cleared, stored = sem("h_in"), sem("w_in"), sem("cleared"), sem("stored")
        v = sem("dve_step")
        tp_done, hT_done = sem("tp_done"), sem("hT_done")
        r_ps = sem("r_ps")
        kvr_ps, kvr_sb, sig_sb = sem("kvr_ps"), sem("kvr_sb"), sem("sig_sb")
        wo_ps, wo_sb, r2_ps, r2_sb = sem("wo_ps"), sem("wo_sb"), sem("r2_ps"), sem("r2_sb")
        kf_ps, rl_sb, kk_sb, vf_ps, vf_sb = sem("kf_ps"), sem("rl_sb"), sem("kk_sb"), sem("vf_ps"), sem("vf_sb")
        w1_ps, hid_sb, lg_ps, lg_sb = sem("w1_ps"), sem("hid_sb"), sem("lg_ps"), sem("lg_sb")
        ex_ps, prod_sb, moe_sb = sem("ex_ps"), sem("prod_sb"), sem("moe_sb")
        dev_sb, sq_sb, var_in, std_in = sem("dev_sb"), sem("sq_sb"), sem("var_in"), sem("std_in")
        ln_in, scan_in = sem("ln_in"), sem("scan_in")
        w = sem("pool_step")
        first_in, max_in, q_in, p_in = sem("first_in"), sem("max_in"), sem("q_in"), sem("p_in")
        inv_in, y_in = sem("inv_in"), sem("y_in")
        gate_in, gT_ps, gT_sb, bd_ps, bd_sb = sem("gate_in"), sem("gT_ps"), sem("gT_sb"), sem("bd_ps"), sem("bd_sb")
        logits_in, out_ready, exp_sb = sem("logits_in"), sem("out_ready"), sem("exp_sb")
        NWIN = 1 + 2 * (3 + 4 + 4) + 2 * 4 + 16 + 3
        block = ctx.enter_context(nc.Block())

        def bank(i):
            return ps[:, i, :]

        def tc(ap):
            return ap.rearrange("p (t c) -> p t c", t=T64)

        def ct(ap):
            return ap.rearrange("p (c t) -> p c t", c=CT)

        def over_c(ap):
            return ap.rearrange("p (t o) -> p t o", o=1).to_broadcast([128, T64, CT])

        def per_c(ap):
            return ap.rearrange("p (c o) -> p c o", o=1).to_broadcast([128, CT, T64])

        @block.sync
        def _(sp):
            sp.dma_start(H, t["hs"].rearrange("g r i s f -> (g r i) (s f)")).then_inc(h_in, 16)
            sp.wait_ge(cleared, 1)
            sp.dma_start(ident, t["t_ident"]).then_inc(w_in, 16)
            for t2 in range(2):
                q = slice(64 * t2, 64 * t2 + 64)
                for i, w in enumerate(("Wk", "Wv", "Wr")):
                    c0 = 128 * i + 64 * t2
                    sp.dma_start(wkvr[q, c0:c0 + 64], t["L0_attn_" + w]).then_inc(w_in, 16)
                sp.dma_start(wo[q, q], t["L0_attn_Wo"]).then_inc(w_in, 16)
                sp.dma_start(wr[q, q], t["L0_attn_Wr_ffn"]).then_inc(w_in, 16)
                sp.dma_start(wk_f[q, :], t["L0_attn_Wk_ffn"]).then_inc(w_in, 16)
                sp.dma_start(w1[q, :], t["L0_ffn_W1"]).then_inc(w_in, 16)
                for dst, w in ((g1, "attn_g1"), (b1, "attn_b1"), (g2, "attn_g2"), (b2, "attn_b2")):
                    sp.dma_start(dst[q, :], t["L0_" + w].rearrange("(c o) -> c o", o=1)).then_inc(w_in, 16)
            for m in range(2):
                h = slice(128 * m, 128 * m + 128)
                sp.dma_start(wv_f[:, 64 * m:64 * m + 64], t["L0_attn_Wv_ffn"][h, :]).then_inc(w_in, 16)
                sp.dma_start(wg[:, E * m:E * m + E], t["L0_ffn_Wg"][h, :]).then_inc(w_in, 16)
                sp.dma_start(b1m[:, m:m + 1], t["L0_ffn_b1"][h].rearrange("(c o) -> c o", o=1)).then_inc(w_in, 16)
                sp.dma_start(wd[:, 512 * m:512 * m + 512].rearrange("p (e c) -> p e c", e=E),
                             t["L0_ffn_Wd"][:, h, :].rearrange("e p c -> p e c")).then_inc(w_in, 16)
            for i in range(16):
                sp.dma_start(bd_diag[E * i:E * i + E, CT * i:CT * i + CT], t["L0_ffn_bd"]).then_inc(w_in, 16)
            for dst, w in ((bg_bc, t["L0_ffn_bg"]),
                           (dec, t["L0_attn_spatial_decay"]), (fst, t["L0_attn_spatial_first"])):
                sp.dma_start(dst, w.rearrange("(o n) -> o n", o=1).to_broadcast([128, dst.shape[1]])).then_inc(w_in, 16)
            for i in range(2):
                c = slice(N // 2 * i, N // 2 * (i + 1))
                sp.wait_ge(out_ready, 4 * (i + 1))
                sp.dma_start(out.rearrange("b t c -> b (t c)")[:, c], A2[:, c]).then_inc(stored, 16)
            sp.wait_ge(stored, 32)

        @block.vector
        def _(dve):
            n, norms = [0], [0]

            def step(ins):
                n[0] += 1
                ins.then_inc(v, 1)
                dve.wait_ge(v, n[0])

            def sums(src, k):
                return nc.vector.tensor_reduce(mean[:, 8 * k:8 * k + 8], tc(src)[:, 8 * k:8 * k + 8], AX.X, ALU.add)

            def layer_norm(src, dst, tmp, done):
                halves = [slice(T64 // 2 * i, T64 // 2 * (i + 1)) for i in range(2)]
                step(nc.vector.tensor_scalar(mean, mean, 1.0 / CT, None, ALU.mult))
                for h in halves:
                    tt(tc(dst)[:, h], tc(src)[:, h], over_c(mean)[:, h], ALU.subtract).then_inc(dev_sb, 1)
                for i, h in enumerate(halves):
                    dve.wait_ge(sq_sb, 2 * norms[0] + i + 1)
                    step(nc.vector.tensor_reduce(var[:, h], tc(tmp)[:, h], AX.X, ALU.add))
                step(nc.vector.tensor_scalar(var, var, 1.0 / CT, 1e-5, ALU.mult, ALU.add))
                norms[0] += 1
                nc.vector.engine_nop().then_inc(var_in, 1)
                dve.wait_ge(std_in, norms[0])
                step(nc.vector.reciprocal(rstd, std))
                for k in range(8):
                    t8 = slice(8 * k, 8 * k + 8)
                    tt(tc(dst)[:, t8], tc(dst)[:, t8], over_c(rstd)[:, t8], ALU.mult).then_inc(done, 1)

            tt = nc.vector.tensor_tensor
            late, early = slice(1, T64), slice(0, T64 - 1)
            nc.vector.memset(wkvr, 0.0)
            nc.vector.memset(wg, 0.0)
            nc.vector.memset(bd_diag, 0.0)
            nc.vector.memset(wo, 0.0)
            nc.vector.memset(wr, 0.0).then_inc(cleared, 1)
            for e in range(E):
                m = nc.vector.memset(rank[:, e:e + 1], float(E - e))
            step(m)
            dve.wait_ge(h_in, 16)
            step(nc.vector.tensor_reduce(mean, tc(H), AX.X, ALU.add))
            layer_norm(H, A1, A2, ln_in)
            dve.wait_ge(w_in, 16 * NWIN)
            step(nc.vector.tensor_scalar(dec, dec, 1.0 / T64, None, ALU.mult))
            step(nc.vector.tensor_scalar(fst, fst, 1.0 / T64, None, ALU.mult))
            nc.vector.engine_nop().then_inc(first_in, 1)
            step(nc.vector.tensor_copy(ct(A3), per_c(dec)))
            step(nc.vector.memset(ct(A3)[:, :, 0:1], NEG))
            for tp in range(TP):
                dve.wait_ge(kvr_ps, tp + 1)
                src = bank(tp % 4)[:, 0:256].rearrange("p (k t c) -> p k c t", k=2, t=2)
                nc.vector.tensor_copy(ct(K)[:, :, 2 * tp:2 * tp + 2], src[:, 0])
                nc.vector.tensor_copy(ct(Vv)[:, :, 2 * tp:2 * tp + 2], src[:, 1]).then_inc(kvr_sb, 1)
            dve.wait_ge(kvr_sb, TP)
            step(nc.vector.tensor_tensor_scan(A2, A3, K, NEG, ALU.add, ALU.max))
            dve.wait_ge(w, 1)
            step(tt(ct(A1)[:, :, late], ct(A4)[:, :, late], ct(A2)[:, :, early], ALU.max))
            step(nc.vector.tensor_copy(ct(A1)[:, :, 0:1], ct(A4)[:, :, 0:1]))
            nc.vector.engine_nop().then_inc(max_in, 1)
            step(tt(A3, A3, A2, ALU.subtract))
            step(tt(ct(A3)[:, :, late], ct(A3)[:, :, late], ct(A2)[:, :, early], ALU.add))
            nc.vector.engine_nop().then_inc(scan_in, 1)
            step(tt(K, K, A2, ALU.subtract))
            nc.vector.engine_nop().then_inc(scan_in, 1)
            dve.wait_ge(exp_sb, 2)
            dve.wait_ge(sig_sb, TP)
            step(nc.vector.tensor_tensor_scan(hT, A3, K, 0.0, ALU.mult, ALU.add))
            nc.vector.engine_nop().then_inc(q_in, 1)
            step(tt(K, K, Vv, ALU.mult))
            step(nc.vector.tensor_tensor_scan(kk, A3, K, 0.0, ALU.mult, ALU.add))
            nc.vector.engine_nop().then_inc(p_in, 1)
            dve.wait_ge(w, 7)
            c16 = [slice(CT // 4 * i, CT // 4 * (i + 1)) for i in range(4)]
            for i in range(5):
                if i < 4:
                    nc.vector.reciprocal(ct(A4)[:, c16[i]], ct(A4)[:, c16[i]]).then_inc(inv_in, 1)
                if i > 0:
                    dve.wait_ge(y_in, i)
                    step(tt(tc(A1)[:, :, c16[i - 1]], tc(R)[:, :, c16[i - 1]],
                            ct(A2).rearrange("p c t -> p t c")[:, :, c16[i - 1]], ALU.mult))
            nc.vector.engine_nop().then_inc(ln_in, 8)
            dve.wait_ge(ln_in, 16)
            for k in range(8):
                dve.wait_ge(wo_ps, k + 1)
                c = slice(512 * k, 512 * k + 512)
                tt(A2[:, c], H[:, c], bank(k), ALU.add).then_inc(wo_sb, 1)
                dve.wait_ge(wo_sb, k + 1)
                step(sums(A2, k))
            layer_norm(A2, A1, A3, ln_in)
            for f in range(32):
                i = f // 4
                dve.wait_ge(rl_sb, f + 1)
                if i >= 2 and f % 4 == 0:
                    dve.wait_ge(vf_ps, i - 1)
                r = rl[:, f % 2 * 512:f % 2 * 512 + 512]
                tt(kk[:, f % 8 * 512:f % 8 * 512 + 512], r, r, ALU.mult).then_inc(kk_sb, 1)
                if f % 4 == 3:
                    for j in ([i - 1] if i else []) + ([7] if i == 7 else []):
                        dve.wait_ge(vf_ps, j + 1)
                        c = slice(512 * j, 512 * j + 512)
                        tt(A3[:, c], R[:, c], bank(6 + j % 2), ALU.mult).then_inc(vf_sb, 1)
                        dve.wait_ge(vf_sb, j + 1)
                        step(tt(A2[:, c], A2[:, c], A3[:, c], ALU.add))
                        step(tt(H[:, c], H[:, c], A2[:, c], ALU.add))
                        step(sums(H, j))
            layer_norm(H, K, Vv, ln_in)
            te = lambda ap: ap.rearrange("p (t e) -> p t e", e=E)
            over_e = lambda ap: ap.rearrange("p (t o) -> p t o", o=1).to_broadcast([128, 8, E])
            over_t = lambda ap: ap.rearrange("p (o e) -> p o e", o=1).to_broadcast([128, 8, E])

            def logits(k):
                c, t8 = slice(64 * k, 64 * k + 64), slice(8 * k, 8 * k + 8)
                dve.wait_ge(lg_ps, k + 1)
                tt(te(lg[:, c]), te(bank(6 + k % 2)[:, 0:64]), over_t(bg_bc), ALU.add).then_inc(lg_sb, 1)
                dve.wait_ge(lg_sb, k + 1)
                step(nc.vector.tensor_reduce(mx[:, t8], te(lg[:, c]), AX.X, ALU.max))
                tt(te(lg[:, c]), te(lg[:, c]), over_e(mx[:, t8]), ALU.subtract).then_inc(logits_in, 1)

            def gates(k):
                c, t8 = slice(64 * k, 64 * k + 64), slice(8 * k, 8 * k + 8)
                l, g, m, d = te(lg[:, c]), te(gate[:, c]), mx[:, t8], sm[:, t8]
                dve.wait_ge(exp_sb, 4 + k + 1)
                step(nc.vector.tensor_reduce(d, l, AX.X, ALU.add))
                step(nc.vector.reciprocal(d, d))
                step(tt(l, l, over_e(d), ALU.mult))
                step(nc.vector.tensor_reduce(m, l, AX.X, ALU.max))
                step(tt(g, l, over_e(m), ALU.is_equal))
                step(tt(g, g, over_t(rank), ALU.mult))
                step(nc.vector.tensor_reduce(d, g, AX.X, ALU.max))
                step(tt(g, g, over_e(d), ALU.is_equal))
                step(tt(g, g, over_e(m), ALU.mult))
                nc.vector.engine_nop().then_inc(gate_in, 1)

            for k in range(8):
                logits(k)
                if k:
                    gates(k - 1)
            gates(7)
            dve.wait_ge(gT_ps, 1)
            nc.vector.tensor_copy(gT, bank(4)).then_inc(gT_sb, 1)
            for i in range(T64):
                k = i // 8
                dve.wait_ge(ex_ps, i + 1)
                p = prod[:, i % 2 * 512:i % 2 * 512 + 512]
                pe_ = p.rearrange("p (e c) -> p e c", e=E)
                tt(pe_, bank(i % 4).rearrange("p (e c) -> p e c", e=E),
                   gate[:, E * i:E * i + E].rearrange("p (e o) -> p e o", o=1).to_broadcast([128, E, CT]),
                   ALU.mult).then_inc(prod_sb, 1)
                dve.wait_ge(prod_sb, i + 1)
                nc.vector.tensor_reduce(Vv[:, CT * i:CT * i + CT], p.rearrange("p (e c) -> p c e", e=E),
                                        AX.X, ALU.add).then_inc(moe_sb, 1)
                if i % 8 == 7:
                    c = slice(512 * k, 512 * k + 512)
                    dve.wait_ge(bd_ps, k + 1)
                    tt(K[:, c], K[:, c], bank(6 + k % 2), ALU.add).then_inc(bd_sb, 1)
                    dve.wait_ge(bd_sb, k + 1)
                    dve.wait_ge(moe_sb, i + 1)
                    step(tt(K[:, c], K[:, c], Vv[:, c], ALU.add))
                    step(sums(K, k))
            layer_norm(K, A2, A3, out_ready)

        @block.tensor
        def _(pe):
            mm = nc.tensor.matmul

            def turn(i, src):
                for k in range(8):
                    pe.wait_ge(ln_in, 8 * i + k + 1)
                    for j in range(4):
                        c0 = 512 * k + 128 * j
                        m = nc.tensor.transpose(bank(k)[:, 128 * j:128 * j + 128], src[:, c0:c0 + 128], ident)
                    m.then_inc(tp_done, 1)

            def pair(tp):
                return hT[:, 128 * tp:128 * tp + 128]

            pe.wait_ge(w_in, 16 * NWIN)
            turn(0, A1)
            pe.wait_ge(hT_done, 8)
            for tp in range(TP):
                if tp >= 4:
                    pe.wait_ge(kvr_sb, tp - 3)
                    pe.wait_ge(sig_sb, tp - 3)
                mm(bank(tp % 4)[:, 0:256], pair(tp), wkvr[:, 0:256], start=True, stop=True).then_inc(kvr_ps, 1)
                mm(bank(4 + tp % 4)[:, 0:128], pair(tp), wkvr[:, 256:384], start=True, stop=True).then_inc(r_ps, 1)
            pe.wait_ge(sig_sb, TP)
            pe.wait_ge(kvr_sb, TP)
            turn(1, A1)
            for k in range(8):
                pe.wait_ge(hT_done, 8 + k + 1)
                for j in range(4):
                    m = mm(bank(k)[:, 128 * j:128 * j + 128], pair(4 * k + j), wo, start=True, stop=True)
                m.then_inc(wo_ps, 1)
            pe.wait_ge(wo_sb, 8)
            turn(2, A1)
            pe.wait_ge(hT_done, 24)
            for k in range(8):
                for j in range(4):
                    m = mm(bank(k)[:, 128 * j:128 * j + 128], pair(4 * k + j), wr, start=True, stop=True)
                m.then_inc(r2_ps, 1)
            pe.wait_ge(r2_sb, 8)

            def hidden(i, w, filled, emptied):
                for k in range(4):
                    f = 4 * i + k
                    t2, m = divmod(k, 2)
                    q = slice(64 * t2, 64 * t2 + 64)
                    if f >= 4:
                        pe.wait_ge(emptied, f - 3)
                    mm(bank(f % 4), w[q, 128 * m:128 * m + 128], hT[q, 512 * i:512 * i + 512],
                       start=True, stop=True).then_inc(filled, 1)

            hidden(0, wk_f, kf_ps, rl_sb)
            for i in range(8):
                if i < 7:
                    hidden(i + 1, wk_f, kf_ps, rl_sb)
                pe.wait_ge(kk_sb, 4 * i + 4)
                if i >= 2:
                    pe.wait_ge(vf_sb, i - 1)
                for j in range(8):
                    for m in range(2):
                        c0 = (4 * (i % 2) + 2 * (j % 2) + m) * 512 + 128 * (j // 2)
                        ins = mm(bank(6 + i % 2)[:, CT * j:CT * j + CT], kk[:, c0:c0 + 128],
                                 wv_f[:, CT * m:CT * m + CT], start=m == 0, stop=m == 1)
                ins.then_inc(vf_ps, 1)
            turn(3, K)
            pe.wait_ge(hT_done, 32)
            hidden(0, w1, w1_ps, hid_sb)
            for i in range(8):
                if i < 7:
                    hidden(i + 1, w1, w1_ps, hid_sb)
                pe.wait_ge(hid_sb, 4 * i + 4)
                if i >= 2:
                    pe.wait_ge(lg_sb, i - 1)
                for j in range(8):
                    for m in range(2):
                        c0 = m * 2 * N + (8 * i + j) * 128
                        ins = mm(bank(6 + i % 2)[:, E * j:E * j + WARM], hid[:, c0:c0 + 128],
                                 wg[:, E * m:E * m + WARM], start=m == 0, stop=m == 1)
                ins.then_inc(lg_ps, 1)
            def experts(i):
                if i >= 4:
                    pe.wait_ge(prod_sb, i - 3)
                for m in range(2):
                    c0 = m * 2 * N + i * 128
                    ins = mm(bank(i % 4), hid[:, c0:c0 + 128], wd[:, 512 * m:512 * m + 512],
                             start=m == 0, stop=m == 1)
                ins.then_inc(ex_ps, 1)

            pe.wait_ge(hid_sb, 32)
            for i in range(4):
                experts(i)
            pe.wait_ge(gate_in, 8)
            for k in range(4):
                m = nc.tensor.transpose(bank(4)[:, 128 * k:128 * k + 128], gate[:, 128 * k:128 * k + 128], ident)
            m.then_inc(gT_ps, 1)
            for i in range(4, T64):
                if i % 8 == 5:
                    k = i // 8
                    pe.wait_ge(gT_sb, 1)
                    if k >= 2:
                        pe.wait_ge(bd_sb, k - 1)
                    mm(bank(6 + k % 2), gT[:, 128 * (k // 2):128 * (k // 2) + 128],
                       bd_diag[:, 512 * (k % 2):512 * (k % 2) + 512], start=True, stop=True).then_inc(bd_ps, 1)
                experts(i)

        @block.gpsimd
        def _(pool):
            n = [0]

            def step(ins):
                n[0] += 1
                ins.then_inc(w, 1)
                pool.wait_ge(w, n[0])

            tt = nc.gpsimd.tensor_tensor
            late, early = slice(1, T64), slice(0, T64 - 1)
            pool.wait_ge(first_in, 1)
            pool.wait_ge(kvr_sb, TP)
            step(tt(ct(A4), ct(K), per_c(fst), ALU.add))
            pool.wait_ge(max_in, 1)
            step(tt(A4, A4, A1, ALU.subtract))
            step(tt(ct(A1)[:, :, late], ct(A2)[:, :, early], ct(A1)[:, :, late], ALU.subtract))
            step(nc.gpsimd.memset(ct(A1)[:, :, 0:1], NEG))
            pool.wait_ge(scan_in, 2)
            pool.wait_ge(exp_sb, 3)
            step(tt(A2, A4, Vv, ALU.mult))
            pool.wait_ge(q_in, 1)
            pool.wait_ge(exp_sb, 4)
            step(tt(ct(hT)[:, :, early], ct(A1)[:, :, late], ct(hT)[:, :, early], ALU.mult))
            step(tt(ct(A4)[:, :, late], ct(A4)[:, :, late], ct(hT)[:, :, early], ALU.add))
            pool.wait_ge(p_in, 1)
            step(tt(ct(kk)[:, :, early], ct(A1)[:, :, late], ct(kk)[:, :, early], ALU.mult))
            step(tt(ct(A2)[:, :, late], ct(A2)[:, :, late], ct(kk)[:, :, early], ALU.add))
            for i in range(4):
                c = slice(N // 4 * i, N // 4 * (i + 1))
                pool.wait_ge(inv_in, i + 1)
                tt(A2[:, c], A2[:, c], A4[:, c], ALU.mult).then_inc(y_in, 1)

        @block.scalar
        def _(act):
            def norm(i, dev, squares):
                for k in range(2):
                    c = slice(N // 2 * k, N // 2 * (k + 1))
                    act.wait_ge(dev_sb, 2 * i + k + 1)
                    nc.scalar.activation(squares[:, c], dev[:, c], ACT.Square).then_inc(sq_sb, 1)
                act.wait_ge(var_in, i + 1)
                nc.scalar.activation(std, var, ACT.Sqrt).then_inc(std_in, 1)

            def turned(i, gain=None, bias=None):
                for k in range(8):
                    act.wait_ge(tp_done, 8 * i + k + 1)
                    o = hT[:, 512 * k:512 * k + 512]
                    if gain is None:
                        nc.scalar.activation(o, bank(k), ACT.Identity).then_inc(hT_done, 1)
                    else:
                        nc.scalar.activation(o, bank(k), ACT.Identity, scale=gain, bias=bias).then_inc(hT_done, 1)

            norm(0, A1, A2)
            act.wait_ge(w_in, 16 * NWIN)
            turned(0, g1, b1)
            for tp in range(TP):
                act.wait_ge(r_ps, tp + 1)
                nc.scalar.activation(R[:, 128 * tp:128 * tp + 128], bank(4 + tp % 4)[:, 0:128],
                                     ACT.Sigmoid).then_inc(sig_sb, 1)
            for i, ap in enumerate((A3, K)):
                act.wait_ge(scan_in, i + 1)
                nc.scalar.activation(ap, ap, ACT.Exp).then_inc(exp_sb, 1)
            for ap, ready in ((A4, 2), (A1, 4)):
                act.wait_ge(w, ready)
                nc.scalar.activation(ap, ap, ACT.Exp).then_inc(exp_sb, 1)
            turned(1)
            norm(1, A1, A3)
            turned(2, g2, b2)
            for k in range(8):
                act.wait_ge(r2_ps, k + 1)
                nc.scalar.activation(R[:, 512 * k:512 * k + 512], bank(k), ACT.Sigmoid).then_inc(r2_sb, 1)
            for f in range(32):
                act.wait_ge(kf_ps, f + 1)
                if f >= 2:
                    act.wait_ge(kk_sb, f - 1)
                nc.scalar.activation(rl[:, f % 2 * 512:f % 2 * 512 + 512], bank(f % 4), ACT.Relu).then_inc(rl_sb, 1)
            norm(2, K, Vv)
            turned(3)

            def soften(k):
                act.wait_ge(logits_in, k + 1)
                nc.scalar.activation(lg[:, 64 * k:64 * k + 64], lg[:, 64 * k:64 * k + 64], ACT.Exp).then_inc(exp_sb, 1)

            for f in range(32):
                i, t2, m = f // 4, f // 2 % 2, f % 2
                act.wait_ge(w1_ps, f + 1)
                c0 = m * 2 * N + i * 1024
                dst = hid[:, c0:c0 + 1024].rearrange("p (j t b) -> p t j b", j=4, t=2)[:, t2]
                nc.scalar.activation(dst, bank(f % 4).rearrange("p (j b) -> p j b", j=4), ACT.Gelu,
                                     bias=b1m[:, m:m + 1]).then_inc(hid_sb, 1)
                if f % 4 == 0 and i >= 2:
                    soften(i - 2)
            soften(6)
            soften(7)
            norm(3, A2, A3)


def build(nc, t, out):
    tokenizer(nc, t)
    tail(nc, t, out)


def laid_out(inputs):
    a = {k: np.asarray(v) for k, v in inputs.items()}
    x = a["x"].reshape(GROUPS_ALL, OCTS, J, 2, HW * HW, 3).transpose(0, 1, 3, 2, 5, 4).reshape(GROUPS_ALL, OCTS, 24, HW * HW)
    x = np.concatenate([x, x[:1]])
    d = {"x": np.concatenate([x, np.zeros_like(x[:, :, :8])], axis=2)}
    d["sw"] = np.stack([a[f"L0_tok_sw{l % LAYERS}"].reshape(CH, CH, 4, 5, 10, 2).transpose(4, 0, 3, 2, 5, 1).reshape(
        10 * CH, 5 * 8 * CH) for l in range(LAYERS + 1)])
    F = a["x"].dtype
    d["fc0_w"] = np.zeros((128, 256), F)
    for q, i, j in np.ndindex(4, 2, J):
        row, col = 32 * q + 12 * i + 3 * j, 128 * i + CH * j
        d["fc0_w"][row:row + 3, col:col + CH] = a["L0_tok_fc0_w"]
    d["cwb"] = np.zeros((LAYERS, 128, 129), F)
    for l in range(LAYERS):
        for j in range(J):
            q = slice(CH * j, CH * j + CH)
            d["cwb"][l, q, q], d["cwb"][l, q, 128] = a[f"L0_tok_cw{l}"].T, a[f"L0_tok_cb{l}"]
    w1, w2 = a["L0_tok_fc1_w"], a["L0_tok_fc2_w"].reshape(64)
    d["fc_w"] = np.zeros((128, FC), F)
    for j in range(J):
        s, jj = divmod(j, 2)
        d["fc_w"][CH * j:CH * j + CH, 128 * s + 64 * jj:128 * s + 64 * jj + 64] = w1
    for jj in range(2):
        for c in (63, 127):
            d["fc_w"][64 * jj:64 * jj + 64, 256 + c + 16 * jj] = w2
    d["fc_b"] = np.stack([np.tile(a["L0_tok_fc0_b"], 4), np.tile(a["L0_tok_fc1_b"], 2),
                          np.repeat(a["L0_tok_fc2_b"], 128)], axis=1)
    d.update({k: v for k, v in a.items() if k.startswith("L0_attn") or k.startswith("L0_ffn")})
    return {k: np.ascontiguousarray(v) for k, v in d.items()}


GROUPS_ALL = GROUPS


def kernel(**inputs):
    import concourse.bacc as bacc
    from concourse.bass_utils import run_bass_kernel_spmd

    nc = bacc.Bacc("TRN2", target_bir_lowering=False, num_devices=1)
    arrays = laid_out(inputs)
    arrays.update({k: np.ascontiguousarray(v.astype(np.float32)) for k, v in dft_tables().items()})
    t = {k: nc.dram_tensor(k, v.shape, F32, kind="ExternalInput").ap() for k, v in arrays.items()}
    t["hs"] = nc.dram_tensor("hs", (GROUPS, PAIRS, 2, 16, 256), F32, kind="Internal").ap()
    out = nc.dram_tensor("out", (B, HW, HW), F32, kind="ExternalOutput").ap()
    build(nc, t, out)
    r = run_bass_kernel_spmd(nc, [arrays], core_ids=[0])
    return r.results[0]["out"]
```
